# Optimizing a Trainium2 kernel written in Bass

```python
import numpy as np
import jax
import jax.numpy as jnp

def _softmax(x, axis=-1):
    return jax.nn.softmax(x, axis=axis)

def _gelu(x):
    return jax.nn.gelu(x, approximate=True)

def _silu(x):
    return jax.nn.silu(x)

def _sigmoid(x):
    return jax.nn.sigmoid(x)

def _layernorm(x, axis=-1, eps=1e-05):
    m = jnp.mean(x, axis=axis, keepdims=True)
    v = jnp.var(x, axis=axis, keepdims=True)
    return (x - m) / jnp.sqrt(v + eps)

def _scatter_add(tgt, idx, src, axis=0):
    return tgt.at[idx].add(src)

def _segment_sum(src, seg, n):
    return jax.ops.segment_sum(src, seg, n)
kernel_name = 'mk_xattn_ffn_d1_seqx_r2_a79cbe'

def setup_inputs(seed: int=0):
    np.random.seed(seed)
    _w = jnp.asarray

    def _rec_inputs():
        import jax
        import jax.numpy as jnp
        _rk = jax.random.key(seed)
        x = 7.22e-05 + 1 * jax.random.normal(jax.random.fold_in(_rk, 1), (16, 224, 512), jnp.float32)
        _lenS = 224 - jax.random.randint(jax.random.fold_in(_rk, 7), (16,), 0, max(1, 224 // 4) + 1, jnp.int32)
        _lenS2 = 750 - jax.random.randint(jax.random.fold_in(_rk, 8), (16,), 0, max(1, 750 // 4) + 1, jnp.int32)
        _ctx_768P = jax.random.normal(jax.random.fold_in(_rk, 11), (16, 16, 384), jnp.float32)
        _ctx_768c = jax.random.dirichlet(jax.random.fold_in(_rk, 511), 0.3 * jnp.ones((16,), jnp.float32), (16, 750))
        _ctx_768t = jnp.einsum('bsk,bkd->bsd', _ctx_768c, _ctx_768P)
        _ctx_768t = _ctx_768t * jax.lax.rsqrt(jnp.mean(jnp.square(_ctx_768t)) + 1e-12) * 0.953939
        ctx_768 = 2.09791e-05 + 1.00001 * (_ctx_768t + 0.3 * jax.random.normal(jax.random.fold_in(_rk, 611), (16, 750, 384), jnp.float32))
        return (x, ctx_768)
    x, ctx_768 = _rec_inputs()

    def _L0_xattn_setup():
        import jax, jax.numpy as jnp
        import numpy as np
        IN_DIM = 512
        CTX_DIM = 384
        NUM_HEADS = 16
        HEAD_DIM = IN_DIM // NUM_HEADS
        SCALE = 1.0 / float(np.sqrt(HEAD_DIM))
        key = jax.random.key(seed)
        ks = jax.random.split(key, 10)
        B, NQ, NKV = (8, 512, 256)
        s_in = 1.0 / float(np.sqrt(IN_DIM))
        s_ctx = 1.0 / float(np.sqrt(CTX_DIM))
        return {'x': jax.random.normal(ks[0], (B, NQ, IN_DIM), dtype=jnp.float32), 'context': jax.random.normal(ks[1], (B, NKV, CTX_DIM), dtype=jnp.float32), 'Wq': jax.random.normal(ks[2], (IN_DIM, IN_DIM), dtype=jnp.float32) * s_in, 'bq': jax.random.normal(ks[3], (IN_DIM,), dtype=jnp.float32) * 0.01, 'Wk': jax.random.normal(ks[4], (IN_DIM, CTX_DIM), dtype=jnp.float32) * s_ctx, 'bk': jax.random.normal(ks[5], (IN_DIM,), dtype=jnp.float32) * 0.01, 'Wv': jax.random.normal(ks[6], (IN_DIM, CTX_DIM), dtype=jnp.float32) * s_ctx, 'bv': jax.random.normal(ks[7], (IN_DIM,), dtype=jnp.float32) * 0.01, 'Wo': jax.random.normal(ks[8], (IN_DIM, IN_DIM), dtype=jnp.float32) * s_in, 'bo': jax.random.normal(ks[9], (IN_DIM,), dtype=jnp.float32) * 0.01}
    _L0_xattn_all = _L0_xattn_setup()
    _L0_xattn_in = {k: v for k, v in _L0_xattn_all.items() if k in ('Wq', 'bq', 'Wk', 'bk', 'Wv', 'bv', 'Wo', 'bo')}
    del _L0_xattn_all

    def _L0_ffn_setup():
        import jax, jax.numpy as jnp
        import numpy as np
        D_MODEL = 512
        D_FF = 2048
        N_EXPERTS = 8
        D_EXPERT = D_FF // N_EXPERTS
        TOP_K = 2
        LB_WEIGHT = 0.01
        B, S = (4, 1024)

        def _top_k_softmax(logits, k):
            vals, _ = jax.lax.top_k(logits, k)
            thresh = vals[..., -1:]
            masked = jnp.where(logits >= thresh, logits, -jnp.inf)
            return jax.nn.softmax(masked, axis=-1)
        key = jax.random.key(seed)
        ks = jax.random.split(key, 8)
        x = jax.random.normal(ks[0], (B, S, D_MODEL), dtype=jnp.float32)
        w1 = jax.random.normal(ks[1], (N_EXPERTS, D_MODEL, D_EXPERT), dtype=jnp.float32) * (1.0 / np.sqrt(D_MODEL))
        b1 = jnp.zeros((N_EXPERTS, D_EXPERT), dtype=jnp.float32)
        w2 = jax.random.normal(ks[2], (N_EXPERTS, D_EXPERT, D_MODEL), dtype=jnp.float32) * (1.0 / np.sqrt(D_EXPERT))
        b2 = jnp.zeros((N_EXPERTS, D_MODEL), dtype=jnp.float32)
        centroids = jax.random.normal(ks[3], (N_EXPERTS, D_MODEL), dtype=jnp.float32) * 0.02
        w_route = jax.random.normal(ks[4], (N_EXPERTS, D_MODEL), dtype=jnp.float32) * (1.0 / np.sqrt(D_MODEL))
        return {'x': x, 'w1': w1, 'b1': b1, 'w2': w2, 'b2': b2, 'centroids': centroids, 'w_route': w_route}
    _L0_ffn_all = _L0_ffn_setup()
    _L0_ffn_in = {k: v for k, v in _L0_ffn_all.items() if k in ('w1', 'b1', 'w2', 'b2', 'centroids', 'w_route')}
    del _L0_ffn_all
    return {'x': x, 'ctx_768': ctx_768, 'L0_xattn_Wq': _L0_xattn_in['Wq'], 'L0_xattn_bq': _L0_xattn_in['bq'], 'L0_xattn_Wk': _L0_xattn_in['Wk'], 'L0_xattn_bk': _L0_xattn_in['bk'], 'L0_xattn_Wv': _L0_xattn_in['Wv'], 'L0_xattn_bv': _L0_xattn_in['bv'], 'L0_xattn_Wo': _L0_xattn_in['Wo'], 'L0_xattn_bo': _L0_xattn_in['bo'], 'L0_ffn_w1': _L0_ffn_in['w1'], 'L0_ffn_b1': _L0_ffn_in['b1'], 'L0_ffn_w2': _L0_ffn_in['w2'], 'L0_ffn_b2': _L0_ffn_in['b2'], 'L0_ffn_centroids': _L0_ffn_in['centroids'], 'L0_ffn_w_route': _L0_ffn_in['w_route']}

def reference(x, ctx_768, L0_xattn_Wq, L0_xattn_bq, L0_xattn_Wk, L0_xattn_bk, L0_xattn_Wv, L0_xattn_bv, L0_xattn_Wo, L0_xattn_bo, L0_ffn_w1, L0_ffn_b1, L0_ffn_w2, L0_ffn_b2, L0_ffn_centroids, L0_ffn_w_route):
    import jax
    import jax.numpy as jnp

    def _L0_xattn_ref(x, context, Wq, bq, Wk, bk, Wv, bv, Wo, bo):
        import jax, jax.numpy as jnp
        import numpy as np
        IN_DIM = 512
        CTX_DIM = 384
        NUM_HEADS = 16
        HEAD_DIM = IN_DIM // NUM_HEADS
        SCALE = 1.0 / float(np.sqrt(HEAD_DIM))
        q = x @ Wq.T + bq
        k = context @ Wk.T + bk
        v = context @ Wv.T + bv
        B, NQ, _ = q.shape
        NKV = k.shape[1]
        q = q.reshape(B, NQ, NUM_HEADS, HEAD_DIM)
        k = k.reshape(B, NKV, NUM_HEADS, HEAD_DIM)
        v = v.reshape(B, NKV, NUM_HEADS, HEAD_DIM)
        attn = jnp.einsum('bihd,bjhd->bhij', q, k) * SCALE
        attn = jax.nn.softmax(attn, axis=-1)
        out = jnp.einsum('bhij,bjhd->bihd', attn, v)
        out = out.reshape(B, NQ, IN_DIM)
        return out @ Wo.T + bo

    def _L0_ffn_ref(x, w1, b1, w2, b2, centroids, w_route):
        import jax, jax.numpy as jnp
        import numpy as np
        D_MODEL = 512
        D_FF = 2048
        N_EXPERTS = 8
        D_EXPERT = D_FF // N_EXPERTS
        TOP_K = 2
        LB_WEIGHT = 0.01
        B, S = (4, 1024)

        def _top_k_softmax(logits, k):
            vals, _ = jax.lax.top_k(logits, k)
            thresh = vals[..., -1:]
            masked = jnp.where(logits >= thresh, logits, -jnp.inf)
            return jax.nn.softmax(masked, axis=-1)
        eps = 1e-12
        x_norm = x / jnp.maximum(jnp.linalg.norm(x, axis=-1, keepdims=True), eps)
        c_norm = centroids / jnp.maximum(jnp.linalg.norm(centroids, axis=-1, keepdims=True), eps)
        cos_scores = jnp.einsum('bsd,ed->bse', x_norm, c_norm)
        route_scores = jnp.einsum('bsd,ed->bse', x, w_route)
        logits = cos_scores + route_scores
        gates = _top_k_softmax(logits, TOP_K)
        h = jax.nn.gelu(jnp.einsum('bsd,edh->bseh', x, w1) + b1, approximate=False)
        expert_out = jnp.einsum('bseh,ehd->bsed', h, w2) + b2
        out = jnp.einsum('bse,bsed->bsd', gates, expert_out)
        return out
    x = x + _L0_xattn_ref(_layernorm(x, axis=-1), ctx_768, L0_xattn_Wq, L0_xattn_bq, L0_xattn_Wk, L0_xattn_bk, L0_xattn_Wv, L0_xattn_bv, L0_xattn_Wo, L0_xattn_bo)
    x = x + _L0_ffn_ref(_layernorm(x, axis=-1), L0_ffn_w1, L0_ffn_b1, L0_ffn_w2, L0_ffn_b2, L0_ffn_centroids, L0_ffn_w_route)
    return x

_drawn_inputs = setup_inputs


def setup_inputs(seed=0):
    import zlib

    import numpy as np

    out = dict(_drawn_inputs(seed))
    spreads = {'L0_ffn_b1': (0.0, 0.1), 'L0_ffn_b2': (0.0, 0.1)}
    factors = {'L0_xattn_bq': 5.055, 'L0_xattn_bk': 8.0, 'L0_xattn_bo': 2.671}
    for name, (base, spread) in spreads.items():
        noise = np.random.default_rng([zlib.crc32(name.encode()), seed]).standard_normal(out[name].shape)
        drawn = base * np.exp(spread * noise) if base else spread * noise
        out[name] = jnp.asarray(drawn.astype(out[name].dtype))
    for name, factor in factors.items():
        out[name] = (out[name] * factor).astype(out[name].dtype)
    return out
```

```python
from contextlib import ExitStack

import concourse.bass as bass
from concourse import mybir

F32 = mybir.dt.float32
F32R = mybir.dt.float32r
ALU = mybir.AluOpType
ACT = mybir.ActivationFunctionType
AX = mybir.AxisListType

P = 128
B, NQ, D = 16, 224, 512
NKV, C = 750, 384
H, HD = 16, 32
SCALE = 1.0 / float(HD) ** 0.5
EPS = 1e-5
DC, CC = D // P, C // P
QT, QP = 2, NQ // 2
KT, KP = 6, NKV // 6
GH = 4
NG = H // GH
NCH = KT // 2
HALF = ((0, 376), (374, 376))
KHALF = ((0, 376), (376, 374))
ONES_ROW = 96

I32 = mybir.dt.int32
RSQRT_SEED = float(0x5F3759DF)
RSQRT_STEPS = 12


def rsqrt(dve, done, before, src, eps, guard, v, y, tmp):
    def link(instruction):
        nonlocal n
        n += 1
        instruction.then_inc(done, 1)
        dve.wait_ge(done, before + n)

    n = 0
    link(dve.tensor_scalar(v, src, eps, None, guard))
    link(dve.tensor_scalar(y.bitcast(I32), v.bitcast(I32), 1, None, ALU.logical_shift_right))
    link(dve.tensor_scalar(y.bitcast(I32), y.bitcast(I32), -1.0, RSQRT_SEED, ALU.mult, ALU.add))
    for _ in range(3):
        link(dve.tensor_tensor(out=tmp, in0=y, in1=y, op=ALU.mult))
        link(dve.scalar_tensor_tensor(out=tmp, in0=tmp, scalar=-0.5, in1=v, op0=ALU.mult, op1=ALU.mult))
        link(dve.scalar_tensor_tensor(out=y, in0=tmp, scalar=1.5, in1=y, op0=ALU.add, op1=ALU.mult))
    assert n == RSQRT_STEPS


def wait_all(eng, *waits):
    counts = [n if isinstance(n, int) else eng.snap(eng.to_reg(n)) for _, n in waits]
    for (semaphore, _), n in zip(waits, counts):
        eng.wait_ge(semaphore, n)


STEP_UNITS = {t: ["den", "K0", "Q", "K1", "mT"] for t in range(4)}
STEP_UNITS[0] = ["den", "K0", "Q", "K1", "mT", "O0", "O1"]
STEP_UNITS[1] = ["den", "K0", "Q", "K1", "mT", "xT0", "xT1"]
STEP_UNITS[2] = ["den", "K0", "V0", "Q", "K1", "mT", "V1", "V2"]
STEP_UNITS[3] = ["den", "K0", "V3", "Q", "K1", "mT", "V4", "V5"]
PROLOGUE = (["xT0", "xT1"] + [k + s for s in ("_0", "_1") for k in ("K0", "K1", "Q")] + ["mT"]
            + [f"V{n}" for n in range(6)])
EPILOGUE = ["den", "O0", "O1"]


def present(b, t, kind):
    if b == "first" and t == 0 and kind in ("den", "O0", "O1"):
        return False
    if b == "last":
        if kind[0] in "xV" or (t >= 2 and kind in ("K0", "K1", "Q")) or (t == 3 and kind == "mT"):
            return False
    return True


def unit_table():
    parts = {"prologue": {(0, k): n for n, k in enumerate(PROLOGUE)},
             "epilogue": {(0, k): n for n, k in enumerate(EPILOGUE)}}
    for b in ("first", "mid", "last"):
        keys = [(t, k) for t in range(4) for k in STEP_UNITS[t] if present(b, t, k)]
        parts[b] = {k: n for n, k in enumerate(keys)}
    base = {"prologue": 0, "first": len(PROLOGUE)}
    base["mid"] = base["first"] + len(parts["first"])
    base["last"] = base["mid"] + (B - 2) * len(parts["mid"])
    base["epilogue"] = base["last"] + len(parts["last"])
    return parts, base


PARTS, BASE = unit_table()
PER_BATCH = len(PARTS["mid"])
assert PER_BATCH % 2 == 0


def misc(part, b, t, kind):
    n = BASE[part] + PARTS[part][(t, kind)]
    if part == "mid":
        return n % 2, (b - 1) * (PER_BATCH // 2) + n // 2
    return n % 2, n // 2


def attention_phase(nc, x, ctxT, wqT, bq, wkT, bk, wvT, bv, woT, bo, ident, x1):
    with ExitStack() as es:
        def sb(name, shape, dt=F32):
            return es.enter_context(nc.sbuf_tensor(name, shape, dt))

        def sem(name):
            return es.enter_context(nc.semaphore(name))

        wk_h, wk_l = sb("wk_h", [P, CC, D], F32R), sb("wk_l", [P, CC, D], F32R)
        wv_h, wv_l = sb("wv_h", [P, CC, D], F32R), sb("wv_l", [P, CC, D], F32R)
        wq_h, wq_l = sb("wq_h", [P, DC, D], F32R), sb("wq_l", [P, DC, D], F32R)
        wo_h, wo_l = sb("wo_h", [P, DC, D], F32R), sb("wo_l", [P, DC, D], F32R)
        bq_s, bk_s, bv_s = sb("bq_s", [P, NG]), sb("bk_s", [P, NG]), sb("bv_s", [P, NG])
        bo_s = sb("bo_s", [P, D])
        id_s = sb("id_s", [P, P])
        ones = sb("ones", [P, HD])
        kst = sb("kst", [P, H, NKV], F32R)
        qst = sb("qst", [P, H, NQ], F32R)
        kh_s, kl_s = sb("kh_s", [P, NKV], F32R), sb("kl_s", [P, NKV], F32R)
        qh_s, ql_s = sb("qh_s", [P, NQ], F32R), sb("ql_s", [P, NQ], F32R)
        ctx_r = sb("ctx_r", [P, 2, NKV])
        ctx_h, ctx_l = sb("ctx_h", [P, CC, NKV], F32R), sb("ctx_l", [P, CC, NKV], F32R)
        xb = sb("xb", [P, QT, D])
        xT_h, xT_l = sb("xT_h", [P, DC, NQ], F32R), sb("xT_l", [P, DC, NQ], F32R)
        stats, mv, rstd = sb("stats", [P, QT, 6]), sb("mv", [P, QT, 2]), sb("rstd", [P, QT])
        ve, rtmp, settled = sb("ve", [P, QT]), sb("rtmp", [P, QT]), sb("settled", [P, 1])
        v01 = sb("v01", [P, KT, 2 * P])
        v23 = sb("v23", [P, 2, KT, 2 * P])
        pr = sb("pr", [P, 2, GH, 2, NQ])
        psum_p = sb("psum_p", [P, GH, NQ])
        mx, mneg = sb("mx", [P, 2 * GH]), sb("mneg", [2 * GH, QP], F32R)
        o_s, rec = sb("o_s", [P, NQ]), sb("rec", [P, NQ])
        oT_h, oT_l = sb("oT_h", [P, NG, NQ], F32R), sb("oT_l", [P, NG, NQ], F32R)

        S = es.enter_context(nc.psum_tensor("S", [P, 3, 512], F32))
        X = es.enter_context(nc.psum_tensor("X", [P, 2, 512], F32))
        O = es.enter_context(nc.psum_tensor("O", [P, 512], F32))
        M = es.enter_context(nc.psum_tensor("M", [P, 2, 512], F32))

        w_in = sem("w_in")
        w_hi, w_lo = sem("w_hi"), sem("w_lo")
        consts = sem("consts")
        ctx_in = [sem(f"ctx_in{c}") for c in range(CC)]
        ctx_hi, ctx_lo = sem("ctx_hi"), sem("ctx_lo")
        x_in, x1_out = sem("x_in"), sem("x1_out")
        bo_added = sem("bo_added")
        ln_stat, ln_var = sem("ln_stat"), sem("ln_var")
        newton = sem("newton")
        xn_done = sem("xn_done")
        misc_full = [sem("misc_full0"), sem("misc_full1")]
        misc_free = [sem("misc_free0"), sem("misc_free1")]
        xT_hi = sem("xT_hi")
        kh_done, qh_done = sem("kh_done"), sem("qh_done")
        kst_in, qst_in = sem("kst_in"), sem("qst_in")
        m_in = sem("m_in")
        x_full, max_done = sem("x_full"), sem("max_done")
        s_full, exp_done = sem("s_full"), sem("exp_done")
        pv_done = sem("pv_done")
        sum_step = sem("sum_step")
        ocopy_done, on_done = sem("ocopy_done"), sem("on_done")
        oh_done, ol_done = sem("oh_done"), sem("ol_done")

        xv = x.rearrange("(b t p) d -> b p t d", t=QT, p=QP)
        x1v = x1.rearrange("(b t p) d -> b p t d", t=QT, p=QP)
        ctxv = ctxT.rearrange("b (c p) n -> b c p n", p=P)
        raw_k = pr[:].rearrange("p a b c n -> p (a b c n)")[:, 0:CC * D]
        raw_q = pr[:].rearrange("p a b c n -> p (a b c n)")[:, CC * D:CC * D + DC * D]
        raw_v = v01[:].rearrange("p a n -> p (a n)")
        raw_o = v23[:].rearrange("p a b n -> p (a b n)")[:, 0:DC * D]

        def v_of(t, par):
            if t < 2:
                return v01[:, :, P * t:P * (t + 1)]
            return v23[:, par, :, P * (t - 2):P * (t - 1)]

        def batches(eng, one):
            one(0, "first", 0)
            with eng.Fori(0, (B - 2) // 2) as pair:
                one(pair * 2 + 1, "mid", 1)
                one(pair * 2 + 2, "mid", 0)
            one(B - 1, "last", 1)

        def has(part, t, kind):
            return (t, kind) in PARTS[part]

        def wait_full(eng, part, b, t, kind):
            bank, count = misc(part, b, t, kind)
            eng.wait_ge(misc_full[bank], count + 1)
            return bank

        def wait_freed(eng, part, b, t, *kinds):
            for semaphore, count in freed(part, b, t, *kinds):
                eng.wait_ge(semaphore, count)

        def freed(part, b, t, *kinds):
            last = dict(misc(part, b, t, kind) for kind in kinds)
            return [(misc_free[bank], count + 1) for bank, count in last.items()]

        def split3(pe, out, lhs, rhs, first, last):
            pe.matmul(out, lhs[0], rhs[0], start=first, stop=False)
            pe.matmul(out, lhs[0], rhs[1], start=False, stop=False)
            return pe.matmul(out, lhs[1], rhs[0], start=False, stop=last)

        with nc.Block() as block:

            @block.sync
            def _(sp):
                for dst, src in ((raw_k, wkT), (raw_q, wqT), (raw_v, wvT), (raw_o, woT)):
                    sp.dma_start(dst.rearrange("p (c n) -> p c n", n=D),
                                 src.rearrange("(c p) n -> p c n", p=P)).then_inc(w_in, 16)
                for dst, src in ((bk_s, bk), (bq_s, bq), (bv_s, bv), (id_s, ident)):
                    sp.dma_start(dst[:, :], src).then_inc(w_in, 16)
                sp.dma_start(bo_s[:, :], bo.partition_broadcast(P)).then_inc(w_in, 16)

                def load_x(b):
                    sp.dma_start(xb[0:QP, :, :], xv[b]).then_inc(x_in, 16)

                def load_ctx(b, c):
                    sp.dma_start(ctx_r[:, c % 2, :], ctxv[b, c]).then_inc(ctx_in[c], 16)

                def stack_q(t):
                    for row, src in ((0, qh_s), (HD, qh_s), (2 * HD, ql_s)):
                        sp.dma_start(qst[row:row + HD, GH * t:GH * (t + 1), :].bitcast(F32),
                                     src[:, :].bitcast(F32)).then_inc(qst_in, 16)

                def stack_k(t):
                    for row, src in ((0, kh_s), (2 * HD, kh_s), (HD, kl_s)):
                        sp.dma_start(kst[row:row + HD, GH * t:GH * (t + 1), :].bitcast(F32),
                                     src[:, :].bitcast(F32)).then_inc(kst_in, 16)

                def put_max(t):
                    sp.dma_start(qst[ONES_ROW:ONES_ROW + 1, GH * t:GH * (t + 1), :].bitcast(F32),
                                 mneg[:, :].bitcast(F32)).then_inc(m_in, 16)

                load_ctx(0, 0)
                load_ctx(0, 1)
                load_x(0)
                sp.wait_ge(ctx_hi, 1)
                sp.wait_ge(ctx_lo, 1)
                load_ctx(0, 2)
                for g in range(2):
                    wait_all(sp, (kh_done, 2 * (g + 1)), *freed("prologue", 0, 0, f"K0_{g}", f"K1_{g}"))
                    stack_k(g)
                    wait_all(sp, (qh_done, g + 1), *freed("prologue", 0, 0, f"Q_{g}"))
                    stack_q(g)
                sp.wait_ge(consts, 5)
                wait_freed(sp, "prologue", 0, 0, "mT")
                put_max(0)

                def one(b, part, par):
                    for t in range(NG):
                        g = 4 * b + t
                        if t == 0 and part != "first":
                            wait_full(sp, "mid", b - 1, 1, "xT1")
                            load_x(b - 1)
                        if t == 0 and part != "last":
                            wait_all(sp, (ctx_hi, CC * (b + 1)), (ctx_lo, CC * (b + 1)))
                            load_ctx(b + 1, 0)
                            load_ctx(b + 1, 1)
                        if t == 1 and part != "last":
                            if part == "first":
                                wait_full(sp, "prologue", 0, 0, "xT1")
                            else:
                                sp.wait_ge(x1_out, 16 * b)
                            load_x(b + 1)
                        if has(part, t, "Q"):
                            done = [] if part == "first" and t < 2 else [(s_full, 12 * (g - 1))]
                            wait_all(sp, (qh_done, g + 3), *freed(part, b, t, "Q"), *done)
                            stack_q((t + 2) % NG)
                            wait_all(sp, (kh_done, 2 * (g + 3)), *freed(part, b, t, "K0", "K1"))
                            stack_k((t + 2) % NG)
                        if has(part, t, "mT"):
                            wait_all(sp, *freed(part, b, t, "mT"))
                            put_max((t + 1) % NG)
                        if t == 1 and part != "last":
                            wait_all(sp, (ctx_hi, CC * (b + 1) + 1), (ctx_lo, CC * (b + 1) + 1))
                            load_ctx(b + 1, 2)
                        if t == 0 and part != "first":
                            wait_all(sp, *freed(part, b, t, "O0", "O1"))
                            sp.dma_start(x1v[b - 1], xb[0:QP, :, :]).then_inc(x1_out, 16)

                batches(sp, one)
                sp.wait_ge(x1_out, 16 * (B - 1))
                load_x(B - 1)
                wait_freed(sp, "epilogue", 0, 0, "O0", "O1")
                sp.dma_start(x1v[B - 1], xb[0:QP, :, :]).then_inc(x1_out, 16)
                sp.wait_ge(x1_out, 16 * B)

            @block.gpsimd
            def _(pool):
                def ctx_lo_part(b, c):
                    pool.wait_ge(ctx_hi, CC * b + c + 1)
                    pool.tensor_tensor(out=ctx_l[:, c, :], in0=ctx_r[:, c % 2, :], in1=ctx_h[:, c, :],
                                       op=ALU.subtract).then_inc(ctx_lo, 1)

                def add_chunk(g, p, buf):
                    pool.wait_ge(exp_done, 12 * g + 4 * p + 4)
                    tiles = [pr[0:KP, buf, :, i, :] for i in range(2)]
                    if p == 0:
                        pool.tensor_tensor(out=psum_p[0:KP, :, :], in0=tiles[0], in1=tiles[1],
                                           op=ALU.add).then_inc(sum_step, 1)
                        return
                    for i in range(2):
                        pool.wait_ge(sum_step, 5 * g + 2 * p - 1 + i)
                        pool.tensor_tensor(out=psum_p[0:KP, :, :], in0=psum_p[0:KP, :, :], in1=tiles[i],
                                           op=ALU.add).then_inc(sum_step, 1)

                def add_bo(n):
                    for qt in range(QT):
                        pool.tensor_tensor(out=xb[0:QP, qt, :], in0=xb[0:QP, qt, :], in1=bo_s[0:QP, :],
                                           op=ALU.add).then_inc(bo_added, 1)

                for c in range(2):
                    ctx_lo_part(0, c)
                ctx_lo_part(0, 2)

                def one(b, part, par):
                    for t in range(NG):
                        g = 4 * b + t
                        if t == 2 and part != "last":
                            ctx_lo_part(b + 1, 2)
                        if has(part, t, "den"):
                            wait_full(pool, part, b, t, "den")
                        add_chunk(g, 0, (3 * t) % 2)
                        if t == 0 and part != "first":
                            pool.wait_ge(x_in, 16 * (2 * b + 1))
                            add_bo(b)
                        add_chunk(g, 1, (3 * t + 1) % 2)
                        if t == 1 and part != "last":
                            ctx_lo_part(b + 1, 0)
                            ctx_lo_part(b + 1, 1)
                        add_chunk(g, 2, (3 * t + 2) % 2)

                batches(pool, one)
                pool.wait_ge(x_in, 16 * 2 * B)
                add_bo(B)

            @block.scalar
            def _(act):
                def w_split(dst, raw, scale, n):
                    act.wait_ge(w_in, 16 * 9)
                    act.activation(dst[:, :, :], raw.rearrange("p (c n) -> p c n", n=D), ACT.Copy,
                                   scale=scale).then_inc(w_hi, 1)

                def ctx_hi_part(b, c):
                    act.wait_ge(ctx_in[c], 16 * (b + 1))
                    act.activation(ctx_h[:, c, :], ctx_r[:, c % 2, :], ACT.Copy).then_inc(ctx_hi, 1)

                def xT_part(part, b, t, i):
                    bank = wait_full(act, part, b, t, f"xT{i}")
                    act.activation(xT_h[:, 2 * i:2 * i + 2, :],
                                   M[:, bank, 0:2 * NQ].rearrange("p (c n) -> p c n", c=2),
                                   ACT.Copy).then_inc(xT_hi, 1)

                def k_hi(part, b, t, kind, g, tg, i):
                    off, w = KHALF[i]
                    bank = wait_full(act, part, b, t, kind)
                    act.activation(kh_s[:, off:off + w], M[:, bank, 0:w], ACT.Identity,
                                   bias=bk_s[:, tg:tg + 1]).then_inc(kh_done, 1)

                def q_hi(part, b, t, kind, g, tg):
                    bank = wait_full(act, part, b, t, kind)
                    act.activation(qh_s[:, :], M[:, bank, 0:NQ], ACT.Identity,
                                   bias=bq_s[:, tg:tg + 1]).then_inc(qh_done, 1)

                def max_out(part, b, t):
                    bank, _ = misc(part, b, t, "mT")
                    wait_full(act, part, b, t, "mT")
                    act.activation(mneg[:, :], M[0:2 * GH, bank, 0:QP], ACT.Copy,
                                   scale=-1.0).then_inc(misc_free[bank], 1)

                def v_out(part, b, t, kind, kt, par):
                    bank = wait_full(act, part, b, t, kind)
                    act.activation(v01[0:KP, kt, :], M[0:KP, bank, 0:2 * P], ACT.Copy)
                    act.activation(v23[0:KP, par, kt, :], M[0:KP, bank, 2 * P:4 * P],
                                   ACT.Copy).then_inc(misc_free[bank], 1)

                w_split(wk_h, raw_k, 1.0, 0)
                ctx_hi_part(0, 0)
                ctx_hi_part(0, 1)
                w_split(wq_h, raw_q, SCALE, 1)
                w_split(wv_h, raw_v, 1.0, 2)
                act.wait_ge(ctx_lo, 1)
                ctx_hi_part(0, 2)
                w_split(wo_h, raw_o, 1.0, 3)
                xT_part("prologue", 0, 0, 0)
                xT_part("prologue", 0, 0, 1)
                act.wait_ge(consts, 5)
                for g in range(2):
                    if g:
                        act.wait_ge(kst_in, 48 * g)
                    k_hi("prologue", 0, 0, f"K0_{g}", g, g, 0)
                    k_hi("prologue", 0, 0, f"K1_{g}", g, g, 1)
                    if g:
                        act.wait_ge(qst_in, 48 * g)
                    q_hi("prologue", 0, 0, f"Q_{g}", g, g)
                max_out("prologue", 0, 0)
                act.wait_ge(w_lo, 4)
                for kt in range(KT):
                    v_out("prologue", 0, 0, f"V{kt}", kt, 0)

                def exps(g, t, part, p, j):
                    buf = (3 * t + p) % 2
                    n = 12 * g + 4 * p + j
                    if j == 0 and not (part == "first" and t == 0 and p < 2):
                        act.wait_ge(pv_done, 3 * g + p - 1)
                        act.wait_ge(sum_step, (5 * g - 2, 5 * g, 5 * g + 1)[p])
                    act.wait_ge(s_full, n + 1)
                    act.activation(pr[0:KP, buf, j, :, :],
                                   S[0:KP, (4 * p + j) % 3, 0:2 * NQ].rearrange("p (i n) -> p i n", i=2),
                                   ACT.Exp).then_inc(exp_done, 1)

                def o_copy(g):
                    act.wait_ge(pv_done, 3 * g + 3)
                    act.activation(o_s[:, :], O[:, 0:NQ], ACT.Copy).then_inc(ocopy_done, 1)

                def o_hi(g, t):
                    act.wait_ge(on_done, g + 1)
                    act.activation(oT_h[:, t, :], o_s[:, :], ACT.Identity, bias=bv_s[:, t:t + 1]).then_inc(oh_done, 1)

                def one(b, part, par):
                    for t in range(NG):
                        g = 4 * b + t
                        before = part != "first" or t > 0
                        project = has(part, t, "Q")
                        exps(g, t, part, 0, 0)
                        exps(g, t, part, 0, 1)
                        if before:
                            if part != "first" or t > 1:
                                act.wait_ge(ol_done, g - 1)
                            o_copy(g - 1)
                        if t == 2 and part != "last":
                            ctx_hi_part(b + 1, 2)
                        exps(g, t, part, 0, 2)
                        exps(g, t, part, 0, 3)
                        if project:
                            act.wait_ge(kst_in, 48 * (g + 2))
                            k_hi(part, b, t, "K0", g + 2, (t + 2) % NG, 0)
                        exps(g, t, part, 1, 0)
                        if before:
                            if t == 1 and part != "first":
                                wait_full(act, part, b, 0, "O1")
                            o_hi(g - 1, (t - 1) % NG)
                        if t == 2 and part != "last":
                            act.wait_ge(pv_done, 3 * g)
                            v_out(part, b, t, "V0", 0, 1 - par)
                        if t == 3 and part != "last":
                            v_out(part, b, t, "V3", 3, 1 - par)
                        exps(g, t, part, 1, 1)
                        if project:
                            act.wait_ge(qst_in, 48 * (g + 2))
                            q_hi(part, b, t, "Q", g + 2, (t + 2) % NG)
                        exps(g, t, part, 1, 2)
                        if project:
                            k_hi(part, b, t, "K1", g + 2, (t + 2) % NG, 1)
                        exps(g, t, part, 1, 3)
                        if t == 1 and part != "last":
                            wait_full(act, part, b, t, "K1")
                            ctx_hi_part(b + 1, 0)
                        exps(g, t, part, 2, 0)
                        if t == 1 and part != "last":
                            ctx_hi_part(b + 1, 1)
                        exps(g, t, part, 2, 1)
                        if has(part, t, "mT"):
                            act.wait_ge(m_in, 16 * (g + 1))
                            max_out(part, b, t)
                        for i in range(2):
                            if t == 1 and part != "last":
                                wait_full(act, part, b, t, "Q")
                                xT_part(part, b, t, i)
                            if t >= 2 and part != "last":
                                kt = 3 * (t - 2) + 1 + i
                                v_out(part, b, t, f"V{kt}", kt, 1 - par)
                            exps(g, t, part, 2, 2 + i)

                batches(act, one)
                g = 4 * B - 1
                act.wait_ge(ol_done, g)
                o_copy(g)
                o_hi(g, NG - 1)

            @block.vector
            def _(dve):
                dve.memset(ones[:, :], 1.0).then_inc(consts, 1)
                dve.memset(kst[ONES_ROW:P, :, :].bitcast(F32), 0.0).then_inc(consts, 1)
                dve.memset(qst[ONES_ROW:P, :, :].bitcast(F32), 0.0).then_inc(consts, 1)
                dve.wait_ge(consts, 2)
                dve.memset(kst[ONES_ROW:ONES_ROW + 1, :, :].bitcast(F32), 1.0).then_inc(consts, 1)
                dve.wait_ge(w_in, 16 * 9)
                dve.tensor_scalar(bq_s[:, :], bq_s[:, :], SCALE, None, ALU.mult).then_inc(consts, 1)

                def w_rest(dst, hi, raw, scale, n):
                    dve.wait_ge(w_hi, n)
                    dve.scalar_tensor_tensor(out=dst[:, :, :], in0=raw.rearrange("p (c n) -> p c n", n=D),
                                             scalar=scale, in1=hi[:, :, :], op0=ALU.mult,
                                             op1=ALU.subtract).then_inc(w_lo, 1)

                def ln_stats(n):
                    for qt in range(QT):
                        dve.bn_stats(stats[0:QP, qt, :], xb[0:QP, qt, :]).then_inc(ln_stat, 1)
                    dve.wait_ge(ln_stat, QT * (n + 1))
                    dve.tensor_copy(settled[:, :], ones[:, 0:1])
                    for qt in range(QT):
                        dve.bn_aggr(mv[0:QP, qt, :], stats[0:QP, qt, :]).then_inc(ln_var, 1)

                def ln_apply(n):
                    dve.wait_ge(ln_var, QT * (n + 1))
                    rsqrt(dve, newton, RSQRT_STEPS * n, mv[0:QP, :, 1], EPS, ALU.add, ve[0:QP, :], rstd[0:QP, :], rtmp[0:QP, :])
                    for qt in range(QT):
                        dve.tensor_scalar(xb[0:QP, qt, :], xb[0:QP, qt, :], mv[0:QP, qt, 0:1],
                                          rstd[0:QP, qt:qt + 1], ALU.subtract, ALU.mult).then_inc(xn_done, 1)

                def xT_rest(part, b, t, i, n):
                    bank, _ = misc(part, b, t, f"xT{i}")
                    dve.wait_ge(xT_hi, n)
                    dve.tensor_tensor(out=xT_l[:, 2 * i:2 * i + 2, :],
                                      in0=M[:, bank, 0:2 * NQ].rearrange("p (c n) -> p c n", c=2),
                                      in1=xT_h[:, 2 * i:2 * i + 2, :],
                                      op=ALU.subtract).then_inc(misc_free[bank], 1)

                def k_lo(part, b, t, kind, g, tg, i):
                    off, w = KHALF[i]
                    bank, _ = misc(part, b, t, kind)
                    dve.wait_ge(kh_done, 2 * g + i + 1)
                    dve.scalar_tensor_tensor(out=kl_s[:, off:off + w], in0=M[:, bank, 0:w], scalar=bk_s[:, tg:tg + 1],
                                             in1=kh_s[:, off:off + w], op0=ALU.add,
                                             op1=ALU.subtract).then_inc(misc_free[bank], 1)

                def q_lo(part, b, t, kind, g, tg):
                    bank, _ = misc(part, b, t, kind)
                    dve.wait_ge(qh_done, g + 1)
                    dve.scalar_tensor_tensor(out=ql_s[:, :], in0=M[:, bank, 0:NQ], scalar=bq_s[:, tg:tg + 1],
                                             in1=qh_s[:, :], op0=ALU.add,
                                             op1=ALU.subtract).then_inc(misc_free[bank], 1)

                def maximum(g, u):
                    dve.wait_ge(x_full, 8 * g + u + 1)
                    dve.tensor_reduce(mx[0:QP, u:u + 1], X[0:QP, :, 0:HALF[0][1]], AX.XY,
                                      ALU.max).then_inc(max_done, 1)

                w_rest(wk_l, wk_h, raw_k, 1.0, 1)
                dve.wait_ge(x_in, 16)
                ln_stats(0)
                w_rest(wq_l, wq_h, raw_q, SCALE, 2)
                ln_apply(0)
                w_rest(wv_l, wv_h, raw_v, 1.0, 3)
                w_rest(wo_l, wo_h, raw_o, 1.0, 4)
                xT_rest("prologue", 0, 0, 0, 1)
                xT_rest("prologue", 0, 0, 1, 2)
                for g in range(2):
                    if g:
                        dve.wait_ge(kst_in, 48 * g)
                    k_lo("prologue", 0, 0, f"K0_{g}", g, g, 0)
                    k_lo("prologue", 0, 0, f"K1_{g}", g, g, 1)
                    if g:
                        dve.wait_ge(qst_in, 48 * g)
                    q_lo("prologue", 0, 0, f"Q_{g}", g, g)
                for u in range(2 * GH):
                    maximum(0, u)

                def normalise(part, b, t, g):
                    bank, count = misc(part, b, t, "den")
                    wait_full(dve, part, b, t, "den")
                    dve.reciprocal(rec[:, :], M[:, bank, 0:NQ]).then_inc(misc_free[bank], 1)
                    dve.wait_ge(misc_free[bank], count + 1)
                    dve.wait_ge(ocopy_done, g + 1)
                    dve.tensor_tensor(out=o_s[:, :], in0=o_s[:, :], in1=rec[:, :], op=ALU.mult).then_inc(on_done, 1)

                def o_lo(g, t):
                    dve.wait_ge(oh_done, g + 1)
                    dve.scalar_tensor_tensor(out=oT_l[:, t, :], in0=o_s[:, :], scalar=bv_s[:, t:t + 1],
                                             in1=oT_h[:, t, :], op0=ALU.add, op1=ALU.subtract).then_inc(ol_done, 1)

                def residual(part, b, t, qt, n):
                    bank = wait_full(dve, part, b, t, f"O{qt}")
                    dve.wait_ge(bo_added, QT * n + qt + 1)
                    dve.tensor_tensor(out=xb[0:QP, qt, :], in0=M[0:QP, bank, :], in1=xb[0:QP, qt, :],
                                      op=ALU.add).then_inc(misc_free[bank], 1)

                def one(b, part, par):
                    for t in range(NG):
                        g = 4 * b + t
                        before = part != "first" or t > 0
                        project = has(part, t, "Q")
                        ahead = has(part, t, "mT")
                        if ahead:
                            if t == 0 and part == "first":
                                wait_full(dve, "prologue", 0, 0, "mT")
                            elif t == 0:
                                wait_full(dve, "mid", b - 1, 3, "mT")
                            else:
                                wait_full(dve, part, b, t - 1, "mT")
                            for u in range(3):
                                maximum(g + 1, u)
                        if before:
                            normalise(part, b, t, g - 1)
                        if ahead:
                            maximum(g + 1, 3)
                        if project:
                            dve.wait_ge(kst_in, 48 * (g + 2))
                            k_lo(part, b, t, "K0", g + 2, (t + 2) % NG, 0)
                        if t == 1 and part != "last":
                            dve.wait_ge(x_in, 16 * (2 * b + 2))
                            ln_stats(b + 1)
                        if ahead:
                            maximum(g + 1, 4)
                        if before:
                            o_lo(g - 1, (t - 1) % NG)
                        if project:
                            dve.wait_ge(qst_in, 48 * (g + 2))
                            q_lo(part, b, t, "Q", g + 2, (t + 2) % NG)
                        if ahead:
                            maximum(g + 1, 5)
                        if project:
                            k_lo(part, b, t, "K1", g + 2, (t + 2) % NG, 1)
                        if ahead:
                            maximum(g + 1, 6)
                            maximum(g + 1, 7)
                        if t == 1 and part != "last":
                            ln_apply(b + 1)
                            for i in range(2):
                                xT_rest(part, b, t, i, 2 * (b + 1) + i + 1)
                        if t == 0 and part != "first":
                            for qt in range(QT):
                                residual(part, b, t, qt, b - 1)

                batches(dve, one)
                normalise("epilogue", 0, 0, 4 * B - 1)
                o_lo(4 * B - 1, NG - 1)
                for qt in range(QT):
                    residual("epilogue", 0, 0, qt, B - 1)

            @block.tensor
            def _(pe):
                def claim(part, b, t, kind):
                    bank, count = misc(part, b, t, kind)
                    if part != "prologue" or count > 0:
                        pe.wait_ge(misc_free[bank], count)
                    return bank, misc_full[bank]

                def transpose_x(part, b, t, i, n):
                    bank, full = claim(part, b, t, f"xT{i}")
                    pe.wait_ge(xn_done, QT * (n + 1))
                    for c in range(2):
                        for qt in range(QT):
                            o = c * NQ + qt * QP
                            last = pe.transpose(M[:, bank, o:o + QP], xb[0:QP, qt, P * (2 * i + c):P * (2 * i + c + 1)],
                                                id_s[0:QP, 0:QP])
                    last.then_inc(full, 1)

                def project_k(part, b, t, kind, tg, i):
                    off, w = KHALF[i]
                    bank, full = claim(part, b, t, kind)
                    cols = slice(P * tg, P * (tg + 1))
                    for c in range(CC):
                        last = split3(pe, M[:, bank, 0:w], (wk_h[:, c, cols], wk_l[:, c, cols]),
                                      (ctx_h[:, c, off:off + w], ctx_l[:, c, off:off + w]), c == 0, c == CC - 1)
                    last.then_inc(full, 1)

                def project_q(part, b, t, kind, tg):
                    bank, full = claim(part, b, t, kind)
                    cols = slice(P * tg, P * (tg + 1))
                    for c in range(DC):
                        last = split3(pe, M[:, bank, 0:NQ], (wq_h[:, c, cols], wq_l[:, c, cols]),
                                      (xT_h[:, c, :], xT_l[:, c, :]), c == 0, c == DC - 1)
                    last.then_inc(full, 1)

                def project_v(part, b, t, kind, kt):
                    bank, full = claim(part, b, t, kind)
                    keys = slice(KP * kt, KP * (kt + 1))
                    for c in range(CC):
                        last = split3(pe, M[0:KP, bank, :], (ctx_h[:, c, keys], ctx_l[:, c, keys]),
                                      (wv_h[:, c, :], wv_l[:, c, :]), c == 0, c == CC - 1)
                    last.then_inc(full, 1)

                def score_for_max(g, tg, u, first=False):
                    h, qt = GH * tg + u // QT, u % QT
                    if u == 0:
                        pe.wait_ge(kst_in, 48 * (g + 1))
                        pe.wait_ge(qst_in, 48 * (g + 1))
                    if not (first and u == 0):
                        pe.wait_ge(max_done, 8 * g + u)
                    for i, (off, w) in enumerate(HALF):
                        last = pe.matmul(X[0:QP, i, 0:w], qst[0:ONES_ROW, h, QP * qt:QP * (qt + 1)],
                                         kst[0:ONES_ROW, h, off:off + w], start=True, stop=True)
                    last.then_inc(x_full, 1)

                def transpose_max(part, b, t, g):
                    bank, full = claim(part, b, t, "mT")
                    pe.wait_ge(max_done, 8 * (g + 1))
                    pe.transpose(M[0:2 * GH, bank, 0:QP], mx[0:QP, :], id_s[0:QP, 0:QP]).then_inc(full, 1)

                pe.wait_ge(w_in, 16 * 9)
                transpose_x("prologue", 0, 0, 0, 0)
                transpose_x("prologue", 0, 0, 1, 0)
                pe.wait_ge(ctx_lo, CC)
                pe.wait_ge(w_lo, 2)
                for g in range(2):
                    project_k("prologue", 0, 0, f"K0_{g}", g, 0)
                    project_k("prologue", 0, 0, f"K1_{g}", g, 1)
                    project_q("prologue", 0, 0, f"Q_{g}", g)
                pe.wait_ge(consts, 5)
                for u in range(2 * GH):
                    score_for_max(0, 0, u, True)
                transpose_max("prologue", 0, 0, 0)
                pe.wait_ge(w_lo, 3)
                for kt in range(KT):
                    project_v("prologue", 0, 0, f"V{kt}", kt)
                pe.wait_ge(w_lo, 4)
                wait_freed(pe, "prologue", 0, 0, "V4")
                wait_freed(pe, "prologue", 0, 0, "V5")

                def score(g, t, part, p, j):
                    n = 12 * g + 4 * p + j
                    if not (part == "first" and t == 0 and 4 * p + j < 3):
                        pe.wait_ge(exp_done, n - 2)
                    for i in range(2):
                        o = KP * (2 * p + i)
                        last = pe.matmul(S[0:KP, (4 * p + j) % 3, NQ * i:NQ * (i + 1)],
                                         kst[:, GH * t + j, o:o + KP], qst[:, GH * t + j, :], start=True, stop=True)
                    last.then_inc(s_full, 1)

                def values(g, t, par, p):
                    pe.wait_ge(exp_done, 12 * g + 4 * p + 4)
                    v = v_of(t, par)
                    for i in range(2):
                        for j in range(GH):
                            last = pe.matmul(O[HD * j:HD * (j + 1), 0:NQ], v[0:KP, 2 * p + i, HD * j:HD * (j + 1)],
                                             pr[0:KP, (3 * t + p) % 2, j, i, :], start=(p == 0 and i == 0),
                                             stop=(p == 2 and i == 1))
                    last.then_inc(pv_done, 1)

                def denominators(part, b, t, g):
                    bank, full = claim(part, b, t, "den")
                    pe.wait_ge(sum_step, 5 * (g + 1))
                    for j in range(GH):
                        last = pe.matmul(M[HD * j:HD * (j + 1), bank, 0:NQ], ones[0:KP, :], psum_p[0:KP, j, :],
                                         start=True, stop=True)
                    last.then_inc(full, 1)

                def project_o(part, b, t, qt, n):
                    bank, full = claim(part, b, t, f"O{qt}")
                    pe.wait_ge(ol_done, NG * n)
                    rows = slice(QP * qt, QP * (qt + 1))
                    for c in range(NG):
                        last = split3(pe, M[0:QP, bank, :], (oT_h[:, c, rows], oT_l[:, c, rows]),
                                      (wo_h[:, c, :], wo_l[:, c, :]), c == 0, c == NG - 1)
                    last.then_inc(full, 1)

                def one(b, part, par):
                    for t in range(NG):
                        g = 4 * b + t
                        before = part != "first" or t > 0
                        project = has(part, t, "Q")
                        ahead = has(part, t, "mT")
                        tn = (t + 1) % NG

                        def for_max(u):
                            if ahead:
                                score_for_max(g + 1, tn, u)

                        pe.wait_ge(m_in, 16 * (g + 1))
                        score(g, t, part, 0, 0)
                        for_max(0)
                        score(g, t, part, 0, 1)
                        if before:
                            values(g - 1, (t - 1) % NG, par if t else 1 - par, 2)
                        for_max(1)
                        score(g, t, part, 0, 2)
                        for_max(2)
                        score(g, t, part, 0, 3)
                        if before:
                            denominators(part, b, t, g - 1)
                        for_max(3)
                        if project:
                            if t == 2:
                                pe.wait_ge(ctx_lo, CC * (b + 2))
                            project_k(part, b, t, "K0", (t + 2) % NG, 0)
                        score(g, t, part, 1, 0)
                        if before:
                            pe.wait_ge(ocopy_done, g)
                        if t == 0 and part != "first":
                            wait_freed(pe, "mid", b - 1, 3, "V4")
                            wait_freed(pe, "mid", b - 1, 3, "V5")
                        values(g, t, par, 0)
                        for_max(4)
                        if t == 2 and part != "last":
                            project_v(part, b, t, "V0", 0)
                        if t == 3 and part != "last":
                            project_v(part, b, t, "V3", 3)
                        score(g, t, part, 1, 1)
                        if project:
                            project_q(part, b, t, "Q", (t + 2) % NG)
                        for_max(5)
                        score(g, t, part, 1, 2)
                        if project:
                            project_k(part, b, t, "K1", (t + 2) % NG, 1)
                        for_max(6)
                        score(g, t, part, 1, 3)
                        for_max(7)
                        score(g, t, part, 2, 0)
                        values(g, t, par, 1)
                        score(g, t, part, 2, 1)
                        if ahead:
                            transpose_max(part, b, t, g + 1)
                        for i in range(2):
                            if t == 0 and part != "first":
                                project_o(part, b, t, i, b)
                            if t == 1 and part != "last":
                                transpose_x(part, b, t, i, b + 1)
                            if t >= 2 and part != "last":
                                kt = 3 * (t - 2) + 1 + i
                                project_v(part, b, t, f"V{kt}", kt)
                            score(g, t, part, 2, 2 + i)

                batches(pe, one)
                values(4 * B - 1, NG - 1, 1, 2)
                denominators("epilogue", 0, 0, 4 * B - 1)
                for qt in range(QT):
                    project_o("epilogue", 0, 0, qt, B)


E, DE = 8, 256
NE = D // P
TB = 512
NB = B * NQ // TB
FT = E * DE // P
NORM_EPS2 = 1e-24
PREP_UNITS = 6
LOGITS, GATES = 4, 5
ROUTE_STEPS, ROUTE_EX = 13, 8


def expert_phase(nc, x1, w1, b1, w2, b2, centroids, w_route, ident, gates_dram, out):
    with ExitStack() as es:
        def sb(name, shape, dt=F32):
            return es.enter_context(nc.sbuf_tensor(name, shape, dt))

        def sem(name):
            return es.enter_context(nc.semaphore(name))

        w1_h, w1_l = sb("w1_h", [P, E, DC, DE], F32R), sb("w1_l", [P, E, DC, DE], F32R)
        w2_h, w2_l = sb("w2_h", [P, E, 2, D], F32R), sb("w2_l", [P, E, 2, D], F32R)
        b1_s, b2_s = sb("b1_s", [P, FT]), sb("b2_s", [E, D])
        id_s = sb("id2_s", [P, P])
        css, cve, cinv, ctmp = sb("css", [E, 1]), sb("cve", [E, 1]), sb("cinv", [E, 1]), sb("ctmp", [E, 1])
        rw = sb("rw", [P, DC, 4 * E], F32R)
        xt = sb("xt", [P, NE, TB])
        res = sb("res", [P, NE, TB])
        xT_h, xT_l = sb("bxT_h", [P, 2, DC, TB], F32R), sb("bxT_l", [P, 2, DC, TB], F32R)
        gate_b = sb("gate_b", [P, 4, TB])
        hid = sb("hid", [P, 2, TB])
        hid_h, hid_l = sb("hid_h", [P, 2, TB], F32R), sb("hid_l", [P, 2, TB], F32R)
        squares = sb("squares", [P, TB])
        stats, mv, rstd = sb("bstats", [P, NE, 6]), sb("bmv", [P, NE, 2]), sb("brstd", [P, NE])
        ve, rtmp, settled = sb("bve", [P, NE]), sb("brtmp", [P, NE]), sb("bsettled", [P, 1])
        ss, rinv = sb("ss", [P, NE]), sb("rinv", [P, NE])
        lg_lo, lg = sb("lg_lo", [P, NE, 2 * E]), sb("lg", [P, NE, 2 * E])
        logit, top8 = sb("logit", [P, NE, E]), sb("top8", [P, NE, 8])
        mask, ex, gsum, gates = sb("mask", [P, NE, E]), sb("ex", [P, NE, E]), sb("gsum", [P, NE]), sb("gates", [P, NE, E])
        gT = sb("gT", [E, TB])
        cent, wr = gate_b[0:E, 0, :], gate_b[0:E, 1, :]

        Y = es.enter_context(nc.psum_tensor("Y", [P, NE, 512], F32))
        HP = es.enter_context(nc.psum_tensor("HP", [P, 2, 512], F32))
        M = es.enter_context(nc.psum_tensor("PREP", [P, 2, 512], F32))

        c_in = sem("c_in")
        w_in = [sem("ew_in0"), sem("ew_in1")]
        w_hi, w_lo = sem("ew_hi"), sem("ew_lo")
        cent_ss, cent_step = sem("cent_ss"), sem("cent_step")
        rw_hi = sem("rw_hi")
        x_in, r_in = sem("ex_in"), sem("r_in")
        out_done = sem("out_done")
        ln_stat, ln_var, newton = sem("eln_stat"), sem("eln_var"), sem("enewton")
        xn_done = sem("exn_done")
        ss_done = sem("ss_done")
        prep_full = [sem("prep_full0"), sem("prep_full1")]
        prep_free = [sem("prep_free0"), sem("prep_free1")]
        xT_hi = sem("exT_hi")
        route, ex_done = sem("route"), sem("ex_done")
        gT_out = sem("gT_out")
        gate_in = [sem(f"gate_in{i}") for i in range(4)]
        h_full, gelu_done, gated = sem("h_full"), sem("gelu_done"), sem("gated")
        hh_done, hl_done = sem("hh_done"), sem("hl_done")
        y_done, y_read = sem("y_done"), sem("y_read")

        x1v = x1.rearrange("(k m p) d -> k p m d", m=NE, p=P)
        outv = out.rearrange("(k m p) d -> k p m d", m=NE, p=P)
        res_flat = res[:].rearrange("p m n -> p (m n)")
        pieces = []
        for e in range(E):
            for i, (w, hi, lo, n) in enumerate(((w1, w1_h, w1_l, DE), (w2, w2_h, w2_l, D))):
                slot = res_flat[:, 2 * D * i:2 * D * (i + 1)].rearrange("p (c n) -> p c n", n=n)
                pieces.append((w[e].rearrange("(c p) n -> p c n", p=P), hi[:, e], lo[:, e], slot))

        def prep(k, u):
            return u % 2, 1 + (PREP_UNITS // 2) * k + u // 2

        def prep_filled(eng, k, u):
            bank, count = prep(k, u)
            eng.wait_ge(prep_full[bank], count + 1)
            return bank

        def prep_freed(eng, k, u):
            bank, count = prep(k, u)
            eng.wait_ge(prep_free[bank], count + 1)

        def blocks(eng, one):
            one(0, 0, "first")
            with eng.Fori(0, (NB - 3) // 2) as pair:
                one(pair * 2 + 1, 1, "mid")
                one(pair * 2 + 2, 0, "mid")
            one(NB - 2, 1, "mid")
            one(NB - 1, 0, "last")

        with nc.Block() as block:

            @block.sync
            def _(sp):
                def load_w(n):
                    src, _, _, slot = pieces[n]
                    sp.dma_start(slot, src).then_inc(w_in[n % 2], 16)

                def load_gates(k, e):
                    sp.dma_start(gate_b[:, e % 4, :], gates_dram[k, e].partition_broadcast(P)).then_inc(gate_in[e % 4], 16)

                sp.dma_start(xt[:, :, :], x1v[0]).then_inc(x_in, 16)
                for dst, src in ((cent, centroids), (wr, w_route), (id_s[:, :], ident), (b1_s[:, :], b1), (b2_s[:, :], b2)):
                    sp.dma_start(dst, src).then_inc(c_in, 16)
                load_w(0)
                load_w(1)
                for n in range(2, 6):
                    sp.wait_ge(w_hi, n - 1)
                    sp.wait_ge(w_lo, n - 1)
                    load_w(n)
                prep_freed(sp, 0, GATES)
                sp.dma_start(gates_dram[0], gT[:, :]).then_inc(gT_out, 16)
                sp.wait_ge(gT_out, 16)
                for e in range(4):
                    load_gates(0, e)

                def one(k, par, part):
                    if part == "first":
                        prep_filled(sp, k, DC - 1)
                        sp.wait_ge(ss_done, NE * (k + 1))
                        sp.dma_start(xt[:, :, :], x1v[k + 1]).then_inc(x_in, 16)
                        for n in range(6, len(pieces)):
                            sp.wait_ge(w_hi, n - 1)
                            sp.wait_ge(w_lo, n - 1)
                            load_w(n)
                            if n % 2 and n // 2 + 1 < E:
                                e = n // 2 + 1
                                sp.wait_ge(gated, 2 * (e - 3))
                                load_gates(k, e)
                        sp.wait_ge(w_hi, len(pieces))
                        sp.wait_ge(w_lo, len(pieces))
                        sp.dma_start(res[:, :, :], x1v[0]).then_inc(r_in, 16)
                    else:
                        if part == "mid":
                            bank, count = prep(k, DC - 1)
                            wait_all(sp, (prep_full[bank], count + 1), (ss_done, NE * (k + 1)))
                            sp.dma_start(xt[:, :, :], x1v[k + 1]).then_inc(x_in, 16)
                        sp.wait_ge(out_done, 16 * k)
                        sp.dma_start(res[:, :, :], x1v[k]).then_inc(r_in, 16)
                        for e in range(4, E):
                            sp.wait_ge(gated, FT * k + 2 * (e - 3))
                            load_gates(k, e)
                    if part != "last":
                        prep_freed(sp, k + 1, GATES)
                        sp.dma_start(gates_dram[k + 1], gT[:, :]).then_inc(gT_out, 16)
                        for e in range(4):
                            wait_all(sp, *([(gT_out, 16 * (k + 2))] if e == 0 else []), (gated, FT * k + 2 * (e + 5)))
                            load_gates(k + 1, e)
                    sp.wait_ge(y_read, NE * (k + 1))
                    sp.dma_start(outv[k], res[:, :, :]).then_inc(out_done, 16)

                blocks(sp, one)
                sp.wait_ge(out_done, 16 * NB)

            @block.scalar
            def _(act):
                def w_part(n):
                    _, hi, _, slot = pieces[n]
                    act.wait_ge(w_in[n % 2], 16 * (n // 2 + 1))
                    act.activation(hi, slot, ACT.Copy).then_inc(w_hi, 1)

                def square(k, m, first=False):
                    act.wait_ge(xn_done, NE * k + m + 1)
                    if first:
                        act.wait_ge(cent_ss, 1)
                    else:
                        act.wait_ge(ss_done, NE * k + m)
                    act.activation(squares[:, :], xt[:, m, :], ACT.Square,
                                   accum_out=ss[:, m:m + 1]).then_inc(ss_done, 1)

                def xT_part(k, par, u):
                    bank = prep_filled(act, k, u)
                    act.activation(xT_h[:, par, u, :], M[:, bank, :], ACT.Copy).then_inc(xT_hi, 1)

                def exps(k):
                    act.wait_ge(route, ROUTE_STEPS * k + ROUTE_EX)
                    act.activation(ex[:, :, :], ex[:, :, :], ACT.Exp).then_inc(ex_done, 1)

                def gT_part(k):
                    bank = prep_filled(act, k, GATES)
                    act.activation(gT[:, :], M[0:E, bank, :], ACT.Copy).then_inc(prep_free[bank], 1)

                act.wait_ge(c_in, 16 * 5)
                act.activation(squares[0:E, :], cent, ACT.Square, accum_out=css[:, :]).then_inc(cent_ss, 1)
                for m in range(NE):
                    square(0, m, m == 0)
                for i in range(2):
                    act.wait_ge(prep_full[i], 1)
                    act.activation(rw[:, :, E * i:E * (i + 1)],
                                   M[:, i, 0:DC * E].rearrange("p (c e) -> p c e", e=E), ACT.Copy).then_inc(rw_hi, 1)
                for u in range(DC):
                    xT_part(0, 0, u)
                w_part(0)
                w_part(1)
                exps(0)
                gT_part(0)
                w_part(2)
                w_part(3)

                def gelu(k, f):
                    act.wait_ge(h_full, FT * k + f + 1)
                    act.activation(hid[:, f % 2, :], HP[:, f % 2, :], ACT.Gelu,
                                   bias=b1_s[:, f:f + 1]).then_inc(gelu_done, 1)

                def hid_hi(k, f):
                    act.wait_ge(gated, FT * k + f + 1)
                    act.activation(hid_h[:, f % 2, :], hid[:, f % 2, :], ACT.Copy).then_inc(hh_done, 1)

                def one(k, par, part):
                    ahead = part != "last"
                    for f in range(FT):
                        n = FT * k + f
                        if part != "first" or f >= 2:
                            act.wait_ge(hl_done, n - 1)
                        gelu(k, f)
                        if f:
                            if part != "first" or f >= 3:
                                act.wait_ge(y_done, n - 2)
                            hid_hi(k, f - 1)
                        if part == "first" and f % 2 == 0 and f // 2 + 2 < E:
                            w_part(f + 4)
                            w_part(f + 5)
                        if ahead and f == 1:
                            for m in range(NE):
                                square(k + 1, m)
                        if ahead and f in (2, 3):
                            xT_part(k + 1, 1 - par, 2 * f - 4)
                            xT_part(k + 1, 1 - par, 2 * f - 3)
                        if ahead and f == 8:
                            exps(k + 1)
                        if ahead and f == 11:
                            act.wait_ge(gT_out, 16 * (k + 1))
                            gT_part(k + 1)
                    act.wait_ge(y_done, FT * k + FT - 2)
                    hid_hi(k, FT - 1)

                blocks(act, one)

            @block.vector
            def _(dve):
                def w_rest(n):
                    _, hi, lo, slot = pieces[n]
                    dve.wait_ge(w_hi, n + 1)
                    dve.tensor_tensor(out=lo, in0=slot, in1=hi, op=ALU.subtract).then_inc(w_lo, 1)

                def ln_stats(k):
                    dve.wait_ge(x_in, 16 * (k + 1))
                    for m in range(NE):
                        dve.bn_stats(stats[:, m, :], xt[:, m, :]).then_inc(ln_stat, 1)
                    dve.wait_ge(ln_stat, NE * (k + 1))
                    dve.tensor_copy(settled[:, :], id_s[:, 0:1])
                    for m in range(NE):
                        dve.bn_aggr(mv[:, m, :], stats[:, m, :]).then_inc(ln_var, 1)

                def ln_apply(k):
                    dve.wait_ge(ln_var, NE * (k + 1))
                    rsqrt(dve, newton, RSQRT_STEPS * (2 * k + 1), mv[:, :, 1], EPS, ALU.add,
                          ve[:, :], rstd[:, :], rtmp[:, :])
                    for m in range(NE):
                        dve.tensor_scalar(xt[:, m, :], xt[:, m, :], mv[:, m, 0:1], rstd[:, m:m + 1],
                                          ALU.subtract, ALU.mult).then_inc(xn_done, 1)

                def xT_rest(k, par, u):
                    bank, _ = prep(k, u)
                    dve.wait_ge(xT_hi, DC * k + u + 1)
                    dve.tensor_tensor(out=xT_l[:, par, u, :], in0=M[:, bank, :], in1=xT_h[:, par, u, :],
                                      op=ALU.subtract).then_inc(prep_free[bank], 1)

                def each(ap):
                    return ap.broadcast_to([P, NE, E])

                def route_before(k):
                    done = ROUTE_STEPS * k
                    dve.wait_ge(ss_done, NE * (k + 1))
                    rsqrt(dve, newton, RSQRT_STEPS * (2 * k + 2), ss[:, :], NORM_EPS2, ALU.max,
                          ve[:, :], rinv[:, :], rtmp[:, :])
                    bank = prep_filled(dve, k, LOGITS)
                    _, count = prep(k, LOGITS)
                    L = M[:, bank, 0:NE * 4 * E].rearrange("p (m e) -> p m e", m=NE)
                    dve.tensor_copy(lg_lo[:, :, :], L[:, :, 2 * E:4 * E]).then_inc(route, 1)
                    dve.wait_ge(route, done + 1)
                    dve.tensor_tensor(out=lg[:, :, :], in0=L[:, :, 0:2 * E], in1=lg_lo[:, :, :],
                                      op=ALU.add).then_inc(prep_free[bank], 1)
                    dve.wait_ge(prep_free[bank], count + 1)
                    dve.tensor_tensor(out=logit[:, :, :], in0=lg[:, :, E:2 * E], in1=each(rinv[:, :].unsqueeze(2)),
                                      op=ALU.mult).then_inc(route, 1)
                    dve.wait_ge(route, done + 2)
                    dve.tensor_tensor(out=logit[:, :, :], in0=logit[:, :, :], in1=lg[:, :, 0:E],
                                      op=ALU.add).then_inc(route, 1)
                    dve.wait_ge(route, done + 3)
                    dve.tensor_copy(settled[:, :], id_s[:, 0:1])
                    for m in range(NE):
                        dve.max(top8[:, m, :], logit[:, m, :]).then_inc(route, 1)
                    dve.wait_ge(route, done + 7)
                    dve.tensor_tensor(out=ex[:, :, :], in0=logit[:, :, :], in1=each(top8[:, :, 0:1]),
                                      op=ALU.subtract).then_inc(route, 1)
                    dve.tensor_tensor(out=mask[:, :, :], in0=logit[:, :, :], in1=each(top8[:, :, 1:2]),
                                      op=ALU.is_ge).then_inc(route, 1)

                def route_after(k):
                    done = ROUTE_STEPS * k + 9
                    dve.wait_ge(ex_done, k + 1)
                    dve.wait_ge(route, done)
                    dve.tensor_tensor(out=ex[:, :, :], in0=ex[:, :, :], in1=mask[:, :, :], op=ALU.mult).then_inc(route, 1)
                    dve.wait_ge(route, done + 1)
                    dve.tensor_reduce(gsum[:, :], ex[:, :, :], AX.X, ALU.add).then_inc(route, 1)
                    dve.wait_ge(route, done + 2)
                    dve.reciprocal(gsum[:, :], gsum[:, :]).then_inc(route, 1)
                    dve.wait_ge(route, done + 3)
                    dve.tensor_tensor(out=gates[:, :, :], in0=ex[:, :, :], in1=each(gsum[:, :].unsqueeze(2)),
                                      op=ALU.mult).then_inc(route, 1)

                dve.wait_ge(cent_ss, 1)
                rsqrt(dve, newton, 0, css[:, :], NORM_EPS2, ALU.max, cve[:, :], cinv[:, :], ctmp[:, :])
                dve.tensor_scalar(cent, cent, cinv[:, 0:1], None, ALU.mult).then_inc(cent_step, 1)
                ln_stats(0)
                ln_apply(0)
                for i in range(2):
                    dve.wait_ge(rw_hi, i + 1)
                    dve.tensor_tensor(out=rw[:, :, E * (2 + i):E * (3 + i)],
                                      in0=M[:, i, 0:DC * E].rearrange("p (c e) -> p c e", e=E),
                                      in1=rw[:, :, E * i:E * (i + 1)], op=ALU.subtract).then_inc(prep_free[i], 1)
                for u in range(DC):
                    xT_rest(0, 0, u)
                w_rest(0)
                w_rest(1)
                route_before(0)
                route_after(0)
                w_rest(2)
                w_rest(3)

                def gate(k, f):
                    e = f // 2
                    dve.wait_ge(gelu_done, FT * k + f + 1)
                    if f % 2 == 0:
                        dve.wait_ge(gate_in[e % 4], 16 * (2 * k + e // 4 + 1))
                    dve.tensor_tensor(out=hid[:, f % 2, :], in0=hid[:, f % 2, :], in1=gate_b[:, e % 4, :],
                                      op=ALU.mult).then_inc(gated, 1)

                def hid_lo(k, f):
                    dve.wait_ge(hh_done, FT * k + f + 1)
                    dve.tensor_tensor(out=hid_l[:, f % 2, :], in0=hid[:, f % 2, :], in1=hid_h[:, f % 2, :],
                                      op=ALU.subtract).then_inc(hl_done, 1)

                def one(k, par, part):
                    ahead = part != "last"
                    for f in range(FT):
                        gate(k, f)
                        if f:
                            hid_lo(k, f - 1)
                        if part == "first" and f % 2 == 0 and f // 2 + 2 < E:
                            w_rest(f + 4)
                            w_rest(f + 5)
                        if ahead and f == 0:
                            ln_stats(k + 1)
                        if ahead and f == 1:
                            ln_apply(k + 1)
                        if ahead and f in (3, 4):
                            xT_rest(k + 1, 1 - par, 2 * f - 6)
                            xT_rest(k + 1, 1 - par, 2 * f - 5)
                        if ahead and f == 7:
                            route_before(k + 1)
                        if ahead and f == 9:
                            route_after(k + 1)
                    hid_lo(k, FT - 1)
                    dve.wait_ge(y_done, FT * (k + 1))
                    dve.wait_ge(r_in, 16 * (k + 1))
                    for m in range(NE):
                        dve.tensor_tensor(out=res[:, m, :], in0=Y[:, m, :], in1=res[:, m, :],
                                          op=ALU.add).then_inc(y_read, 1)

                blocks(dve, one)

            @block.tensor
            def _(pe):
                def transpose_x(k, u):
                    bank, count = prep(k, u)
                    pe.wait_ge(prep_free[bank], count)
                    pe.wait_ge(xn_done, NE * (k + 1))
                    for m in range(NE):
                        last = pe.transpose(M[:, bank, P * m:P * (m + 1)], xt[:, m, P * u:P * (u + 1)], id_s[:, :])
                    last.then_inc(prep_full[bank], 1)

                def logits(k, par):
                    bank, count = prep(k, LOGITS)
                    pe.wait_ge(prep_free[bank], count)
                    prep_freed(pe, k, DC - 1)
                    for m in range(NE):
                        tokens = slice(P * m, P * (m + 1))
                        o = 4 * E * m
                        for c in range(DC):
                            pe.matmul(M[:, bank, o:o + 4 * E], xT_h[:, par, c, tokens], rw[:, c, :],
                                      start=c == 0, stop=False)
                            last = pe.matmul(M[:, bank, o:o + 2 * E], xT_l[:, par, c, tokens], rw[:, c, 0:2 * E],
                                             start=False, stop=c == DC - 1)
                    last.then_inc(prep_full[bank], 1)

                def transpose_gates(k):
                    bank, count = prep(k, GATES)
                    pe.wait_ge(prep_free[bank], count)
                    pe.wait_ge(route, ROUTE_STEPS * (k + 1))
                    for m in range(NE):
                        last = pe.transpose(M[0:E, bank, P * m:P * (m + 1)], gates[:, m, :], id_s[:, :])
                    last.then_inc(prep_full[bank], 1)

                pe.wait_ge(c_in, 16 * 5)
                for i, src in enumerate((wr, cent)):
                    if i:
                        pe.wait_ge(cent_step, 1)
                    for c in range(DC):
                        last = pe.transpose(M[:, i, E * c:E * (c + 1)], src[:, P * c:P * (c + 1)], id_s[0:E, 0:E])
                    last.then_inc(prep_full[i], 1)
                for u in range(DC):
                    transpose_x(0, u)
                logits(0, 0)
                transpose_gates(0)

                def up(k, par, f, part):
                    n, e, cols = FT * k + f, f // 2, slice(P * (f % 2), P * (f % 2 + 1))
                    if part != "first" or f >= 2:
                        pe.wait_ge(gelu_done, n - 1)
                    if part == "first" and f % 2 == 0:
                        pe.wait_ge(w_lo, f + 1)
                    for c in range(DC):
                        out_ap = HP[:, f % 2, :]
                        pe.matmul(out_ap, w1_h[:, e, c, cols], xT_h[:, par, c, :], start=c == 0, stop=False)
                        pe.matmul(out_ap, w1_h[:, e, c, cols], xT_l[:, par, c, :], start=False, stop=False)
                        last = pe.matmul(out_ap, w1_l[:, e, c, cols], xT_h[:, par, c, :], start=False, stop=c == DC - 1)
                    last.then_inc(h_full, 1)

                def down(k, f, part):
                    e, j = f // 2, f % 2
                    if f == 0:
                        if part != "first":
                            pe.wait_ge(y_read, NE * k)
                        prep_freed(pe, k, GATES)
                        for m in range(NE):
                            pe.matmul(Y[:, m, :], gT[:, P * m:P * (m + 1)], b2_s[:, :], start=True, stop=False)
                    if part == "first" and f % 2 == 0:
                        pe.wait_ge(w_lo, f + 2)
                    pe.wait_ge(hl_done, FT * k + f + 1)
                    for m in range(NE):
                        tokens = slice(P * m, P * (m + 1))
                        pe.matmul(Y[:, m, :], hid_h[:, f % 2, tokens], w2_h[:, e, j, :], start=False, stop=False)
                        pe.matmul(Y[:, m, :], hid_h[:, f % 2, tokens], w2_l[:, e, j, :], start=False, stop=False)
                        last = pe.matmul(Y[:, m, :], hid_l[:, f % 2, tokens], w2_h[:, e, j, :], start=False,
                                         stop=f == FT - 1)
                    last.then_inc(y_done, 1)

                def one(k, par, part):
                    ahead = part != "last"
                    for f in range(FT):
                        up(k, par, f, part)
                        if f > 1:
                            down(k, f - 2, part)
                        if ahead and f in (2, 3):
                            transpose_x(k + 1, 2 * f - 4)
                            transpose_x(k + 1, 2 * f - 3)
                        if ahead and f == 6:
                            logits(k + 1, 1 - par)
                        if ahead and f == 10:
                            transpose_gates(k + 1)
                    down(k, FT - 2, part)
                    down(k, FT - 1, part)

                blocks(pe, one)


def kernel(**inputs):
    import concourse.bacc as _bacc
    import numpy as np
    from concourse import mybir as _mybir
    from concourse.bass_utils import run_bass_kernel_spmd as _run

    order = np.arange(D).reshape(NG, GH, HD).transpose(0, 2, 1).reshape(-1)
    put = {
        "x": inputs["x"].reshape(B * NQ, D),
        "ctxT": inputs["ctx_768"].transpose(0, 2, 1),
        "wqT": inputs["L0_xattn_Wq"].T[:, order],
        "bq": inputs["L0_xattn_bq"][order].reshape(NG, P).T,
        "wkT": inputs["L0_xattn_Wk"].T[:, order],
        "bk": inputs["L0_xattn_bk"][order].reshape(NG, P).T,
        "wvT": inputs["L0_xattn_Wv"].T,
        "bv": inputs["L0_xattn_bv"].reshape(NG, P).T,
        "woT": inputs["L0_xattn_Wo"].T,
        "bo": inputs["L0_xattn_bo"],
        "ident": np.eye(P, dtype=np.float32),
        "w1": inputs["L0_ffn_w1"],
        "b1": inputs["L0_ffn_b1"].reshape(FT, P).T,
        "w2": inputs["L0_ffn_w2"],
        "b2": inputs["L0_ffn_b2"],
        "centroids": inputs["L0_ffn_centroids"],
        "w_route": inputs["L0_ffn_w_route"],
    }
    put = {name: np.ascontiguousarray(a) for name, a in put.items()}
    nc = _bacc.Bacc("TRN2", target_bir_lowering=False, num_devices=1)
    ap = {name: nc.dram_tensor(name, a.shape, _mybir.dt.from_np(a.dtype), kind="ExternalInput").ap()
          for name, a in put.items()}
    out = nc.dram_tensor("out", (B * NQ, D), F32, kind="ExternalOutput").ap()
    x1 = nc.dram_tensor("x1", (B * NQ, D), F32, kind="Internal").ap()
    gates = nc.dram_tensor("gates_dram", (NB, E, TB), F32, kind="Internal").ap()
    attention_phase(nc, *(ap[n] for n in ("x", "ctxT", "wqT", "bq", "wkT", "bk", "wvT", "bv", "woT", "bo", "ident")), x1)
    expert_phase(nc, x1, *(ap[n] for n in ("w1", "b1", "w2", "b2", "centroids", "w_route", "ident")), gates, out)
    got = _run(nc, [put], core_ids=[0]).results[0]["out"]
    return got.reshape(B, NQ, D)
```

```python
from contextlib import ExitStack

import concourse.bass as bass
from concourse import mybir

F32 = mybir.dt.float32
F32R = mybir.dt.float32r
ALU = mybir.AluOpType
ACT = mybir.ActivationFunctionType
AX = mybir.AxisListType

P = 128
B, NQ, D = 16, 224, 512
NKV, C = 750, 384
H, HD = 16, 32
SCALE = 1.0 / float(HD) ** 0.5
EPS = 1e-5
DC, CC = D // P, C // P
QT, QP = 2, NQ // 2
KT, KP = 6, NKV // 6
GH = 4
NG = H // GH
NCH = KT // 2
HALF = ((0, 376), (374, 376))
KHALF = ((0, 376), (376, 374))
ONES_ROW = 96

I32 = mybir.dt.int32
RSQRT_SEED = float(0x5F3759DF)
RSQRT_STEPS = 12


def rsqrt(dve, done, before, src, eps, guard, v, y, tmp, first=0, last=RSQRT_STEPS):
    steps = [lambda: dve.tensor_scalar(v, src, eps, None, guard),
             lambda: dve.tensor_scalar(y.bitcast(I32), v.bitcast(I32), 1, None, ALU.logical_shift_right),
             lambda: dve.tensor_scalar(y.bitcast(I32), y.bitcast(I32), -1.0, RSQRT_SEED, ALU.mult, ALU.add)]
    for _ in range(3):
        steps += [lambda: dve.tensor_tensor(out=tmp, in0=y, in1=y, op=ALU.mult),
                  lambda: dve.scalar_tensor_tensor(out=tmp, in0=tmp, scalar=-0.5, in1=v, op0=ALU.mult, op1=ALU.mult),
                  lambda: dve.scalar_tensor_tensor(out=y, in0=tmp, scalar=1.5, in1=y, op0=ALU.add, op1=ALU.mult)]
    assert len(steps) == RSQRT_STEPS
    for n in range(first, last):
        if n:
            dve.wait_ge(done, before + n)
        steps[n]().then_inc(done, 1)
    if last == RSQRT_STEPS:
        dve.wait_ge(done, before + last)


def wait_all(eng, *waits):
    counts = [n if isinstance(n, int) else eng.snap(eng.to_reg(n)) for _, n in waits]
    for (semaphore, _), n in zip(waits, counts):
        eng.wait_ge(semaphore, n)


STEP_UNITS = {
    0: ["Q", "K0", "den", "K1", "O0", "O1", "mT"],
    1: ["Q", "K0", "den", "K1", "mT"],
    2: ["xT0", "xT1", "K0", "V0", "den", "Q", "K1", "V1", "V2", "mT"],
    3: ["Q", "K0", "V3", "den", "K1", "V4", "V5", "mT"],
}
PROLOGUE = (["xT0", "xT1"] + [k + s for s in ("_0", "_1") for k in ("K0", "K1", "Q")]
            + [f"V{n}" for n in range(KT - 1)] + ["mT", f"V{KT - 1}"])
EPILOGUE = ["den", "O0", "O1"]


def present(b, t, kind):
    if b == "first" and t == 0 and kind in ("den", "O0", "O1"):
        return False
    if b == "last":
        if kind[0] in "xV" or (t >= 2 and kind in ("K0", "K1", "Q")) or (t == 3 and kind == "mT"):
            return False
    return True


def unit_table():
    parts = {"prologue": {(0, k): n for n, k in enumerate(PROLOGUE)},
             "epilogue": {(0, k): n for n, k in enumerate(EPILOGUE)}}
    for b in ("first", "mid", "last"):
        keys = [(t, k) for t in range(4) for k in STEP_UNITS[t] if present(b, t, k)]
        parts[b] = {k: n for n, k in enumerate(keys)}
    base = {"prologue": 0, "first": len(PROLOGUE)}
    base["mid"] = base["first"] + len(parts["first"])
    base["last"] = base["mid"] + (B - 2) * len(parts["mid"])
    base["epilogue"] = base["last"] + len(parts["last"])
    return parts, base


PARTS, BASE = unit_table()
PER_BATCH = len(PARTS["mid"])
assert PER_BATCH % 2 == 0


def misc(part, b, t, kind):
    n = BASE[part] + PARTS[part][(t, kind)]
    if part == "mid":
        return n % 2, (b - 1) * (PER_BATCH // 2) + n // 2
    return n % 2, n // 2


def attention_phase(nc, x, ctxT, wqT, bq, wkT, bk, wvT, bv, woT, bo, ident, x1):
    with ExitStack() as es:
        def sb(name, shape, dt=F32):
            return es.enter_context(nc.sbuf_tensor(name, shape, dt))

        def sem(name):
            return es.enter_context(nc.semaphore(name))

        wk_h, wk_l = sb("wk_h", [P, CC, D], F32R), sb("wk_l", [P, CC, D], F32R)
        wv_h, wv_l = sb("wv_h", [P, CC, D], F32R), sb("wv_l", [P, CC, D], F32R)
        wq_h, wq_l = sb("wq_h", [P, DC, D], F32R), sb("wq_l", [P, DC, D], F32R)
        wo_h, wo_l = sb("wo_h", [P, DC, D], F32R), sb("wo_l", [P, DC, D], F32R)
        bq_s, bk_s, bv_s = sb("bq_s", [P, NG]), sb("bk_s", [P, NG]), sb("bv_s", [P, NG])
        bo_s = sb("bo_s", [P, D])
        id_s = sb("id_s", [P, P])
        ones = sb("ones", [P, HD])
        kst = sb("kst", [P, H, NKV], F32R)
        qst = sb("qst", [P, H, NQ], F32R)
        kh_s, kl_s = sb("kh_s", [P, NKV], F32R), sb("kl_s", [P, NKV], F32R)
        qh_s, ql_s = sb("qh_s", [P, NQ], F32R), sb("ql_s", [P, NQ], F32R)
        ctx_r = sb("ctx_r", [P, 2, NKV])
        ctx_h, ctx_l = sb("ctx_h", [P, CC, NKV], F32R), sb("ctx_l", [P, CC, NKV], F32R)
        xb = sb("xb", [P, QT, D])
        xT_h, xT_l = sb("xT_h", [P, DC, NQ], F32R), sb("xT_l", [P, DC, NQ], F32R)
        stats, mv, rstd = sb("stats", [P, QT, 6]), sb("mv", [P, QT, 2]), sb("rstd", [P, QT])
        ve, rtmp, settled = sb("ve", [P, QT]), sb("rtmp", [P, QT]), sb("settled", [P, 1])
        v01 = sb("v01", [P, KT, 2 * P])
        v23 = sb("v23", [P, 2, KT, 2 * P])
        pr = sb("pr", [P, 2, GH, 2, NQ])
        psum_p = sb("psum_p", [P, GH, NQ])
        mx, mneg = sb("mx", [P, 2 * GH]), sb("mneg", [2 * GH, QP], F32R)
        o_s, rec = sb("o_s", [P, NQ]), sb("rec", [P, NQ])
        oT_h, oT_l = sb("oT_h", [P, NG, NQ], F32R), sb("oT_l", [P, NG, NQ], F32R)

        S = es.enter_context(nc.psum_tensor("S", [P, 3, 512], F32))
        X = es.enter_context(nc.psum_tensor("X", [P, 2, 512], F32))
        O = es.enter_context(nc.psum_tensor("O", [P, 512], F32))
        M = es.enter_context(nc.psum_tensor("M", [P, 2, 512], F32))

        w_in = [sem(f"w_in_{n}") for n in "kqvo"]
        c_in = sem("c_in")
        cleared = sem("cleared")
        w_hi, w_lo = sem("w_hi"), sem("w_lo")
        consts = sem("consts")
        ctx_in = [sem(f"ctx_in{c}") for c in range(CC)]
        ctx_hi, ctx_lo = sem("ctx_hi"), sem("ctx_lo")
        x_in, x1_out = sem("x_in"), sem("x1_out")
        bo_added = sem("bo_added")
        ln_stat, ln_var = sem("ln_stat"), sem("ln_var")
        newton = sem("newton")
        xn_done = sem("xn_done")
        misc_full = [sem("misc_full0"), sem("misc_full1")]
        misc_free = [sem("misc_free0"), sem("misc_free1")]
        xT_hi = sem("xT_hi")
        kh_done, qh_done = sem("kh_done"), sem("qh_done")
        kst_in, qst_in = sem("kst_in"), sem("qst_in")
        m_in = sem("m_in")
        x_full, max_done = sem("x_full"), sem("max_done")
        s_full, exp_done = sem("s_full"), sem("exp_done")
        pv_done = sem("pv_done")
        sum_step = sem("sum_step")
        ocopy_done, on_done = sem("ocopy_done"), sem("on_done")
        oh_done, ol_done = sem("oh_done"), sem("ol_done")

        xv = x.rearrange("(b t p) d -> b p t d", t=QT, p=QP)
        x1v = x1.rearrange("(b t p) d -> b p t d", t=QT, p=QP)
        ctxv = ctxT.rearrange("b (c p) n -> b c p n", p=P)
        raw_k = pr[:].rearrange("p a b c n -> p (a b c n)")[:, 0:CC * D]
        raw_q = pr[:].rearrange("p a b c n -> p (a b c n)")[:, CC * D:CC * D + DC * D]
        raw_v = v01[:].rearrange("p a n -> p (a n)")
        raw_o = v23[:].rearrange("p a b n -> p (a b n)")[:, 0:DC * D]

        def v_of(t, par):
            if t < 2:
                return v01[:, :, P * t:P * (t + 1)]
            return v23[:, par, :, P * (t - 2):P * (t - 1)]

        def batches(eng, one):
            one(0, "first", 0)
            with eng.Fori(0, (B - 2) // 2) as pair:
                one(pair * 2 + 1, "mid", 1)
                one(pair * 2 + 2, "mid", 0)
            one(B - 1, "last", 1)

        def has(part, t, kind):
            return (t, kind) in PARTS[part]

        def wait_full(eng, part, b, t, kind):
            bank, count = misc(part, b, t, kind)
            eng.wait_ge(misc_full[bank], count + 1)
            return bank

        def wait_freed(eng, part, b, t, *kinds):
            for semaphore, count in freed(part, b, t, *kinds):
                eng.wait_ge(semaphore, count)

        def freed(part, b, t, *kinds):
            last = dict(misc(part, b, t, kind) for kind in kinds)
            return [(misc_free[bank], count + 1) for bank, count in last.items()]

        def split3(pe, out, lhs, rhs, first, last):
            pe.matmul(out, lhs[0], rhs[0], start=first, stop=False)
            pe.matmul(out, lhs[0], rhs[1], start=False, stop=False)
            return pe.matmul(out, lhs[1], rhs[0], start=False, stop=last)

        with nc.Block() as block:

            @block.sync
            def _(sp):
                def load_w(n, dst, src):
                    sp.dma_start(dst.rearrange("p (c n) -> p c n", n=D),
                                 src.rearrange("(c p) n -> p c n", p=P)).then_inc(w_in[n], 16)

                def load_x(b):
                    sp.dma_start(xb[0:QP, :, :], xv[b]).then_inc(x_in, 16)

                def load_ctx(b, c):
                    sp.dma_start(ctx_r[:, c % 2, :], ctxv[b, c]).then_inc(ctx_in[c], 16)

                def stack_q(t):
                    for row, src in ((0, qh_s), (HD, qh_s), (2 * HD, ql_s)):
                        sp.dma_start(qst[row:row + HD, GH * t:GH * (t + 1), :].bitcast(F32),
                                     src[:, :].bitcast(F32)).then_inc(qst_in, 16)

                def stack_k(t):
                    for row, src in ((0, kh_s), (2 * HD, kh_s), (HD, kl_s)):
                        sp.dma_start(kst[row:row + HD, GH * t:GH * (t + 1), :].bitcast(F32),
                                     src[:, :].bitcast(F32)).then_inc(kst_in, 16)

                def put_max(t):
                    sp.dma_start(qst[ONES_ROW:ONES_ROW + 1, GH * t:GH * (t + 1), :].bitcast(F32),
                                 mneg[:, :].bitcast(F32)).then_inc(m_in, 16)

                load_w(0, raw_k, wkT)
                load_ctx(0, 0)
                load_ctx(0, 1)
                load_x(0)
                for dst, src in ((id_s[:, :], ident), (bk_s[:, :], bk), (bq_s[:, :], bq), (bv_s[:, :], bv),
                                 (bo_s[:, :], bo.partition_broadcast(P))):
                    sp.dma_start(dst, src).then_inc(c_in, 16)
                load_w(1, raw_q, wqT)
                sp.wait_ge(ctx_hi, 1)
                sp.wait_ge(ctx_lo, 1)
                load_ctx(0, 2)
                load_w(2, raw_v, wvT)
                load_w(3, raw_o, woT)
                for g in range(2):
                    wait_all(sp, (kh_done, 2 * (g + 1)), *freed("prologue", 0, 0, f"K0_{g}", f"K1_{g}"))
                    stack_k(g)
                    wait_all(sp, (qh_done, g + 1), *freed("prologue", 0, 0, f"Q_{g}"))
                    stack_q(g)
                sp.wait_ge(consts, 3)
                wait_freed(sp, "prologue", 0, 0, "mT")
                put_max(0)

                def one(b, part, par):
                    for t in range(NG):
                        g = 4 * b + t
                        if t == 0 and part != "first":
                            wait_full(sp, "mid", b - 1, 2, "xT1")
                            load_x(b - 1)
                        if t == 0 and part != "last":
                            wait_all(sp, (ctx_hi, CC * (b + 1)), (ctx_lo, CC * (b + 1)))
                            load_ctx(b + 1, 0)
                            load_ctx(b + 1, 1)
                        if t == 1 and part != "last":
                            if part == "first":
                                wait_full(sp, "prologue", 0, 0, "xT1")
                            else:
                                sp.wait_ge(x1_out, 16 * b)
                            load_x(b + 1)
                        if has(part, t, "Q"):
                            done = [] if part == "first" and t < 2 else [(s_full, 12 * (g - 1))]
                            wait_all(sp, (qh_done, g + 3), *freed(part, b, t, "Q"), *done)
                            stack_q((t + 2) % NG)
                            wait_all(sp, (kh_done, 2 * (g + 3)), *freed(part, b, t, "K0", "K1"))
                            stack_k((t + 2) % NG)
                        if t == 1 and part != "last":
                            wait_all(sp, (ctx_hi, CC * (b + 1) + 1), (ctx_lo, CC * (b + 1) + 1))
                            load_ctx(b + 1, 2)
                        if has(part, t, "mT"):
                            wait_all(sp, *freed(part, b, t, "mT"))
                            put_max((t + 1) % NG)
                        if t == 0 and part != "first":
                            wait_all(sp, *freed(part, b, t, "O0", "O1"))
                            sp.dma_start(x1v[b - 1], xb[0:QP, :, :]).then_inc(x1_out, 16)

                batches(sp, one)
                sp.wait_ge(x1_out, 16 * (B - 1))
                load_x(B - 1)
                wait_freed(sp, "epilogue", 0, 0, "O0", "O1")
                sp.dma_start(x1v[B - 1], xb[0:QP, :, :]).then_inc(x1_out, 16)
                sp.wait_ge(x1_out, 16 * B)

            @block.gpsimd
            def _(pool):
                def ctx_lo_part(b, c):
                    pool.wait_ge(ctx_hi, CC * b + c + 1)
                    pool.tensor_tensor(out=ctx_l[:, c, :], in0=ctx_r[:, c % 2, :], in1=ctx_h[:, c, :],
                                       op=ALU.subtract).then_inc(ctx_lo, 1)

                def add_chunk(g, p, buf):
                    pool.wait_ge(exp_done, 12 * g + 4 * p + 4)
                    tiles = [pr[0:KP, buf, :, i, :] for i in range(2)]
                    if p == 0:
                        pool.tensor_tensor(out=psum_p[0:KP, :, :], in0=tiles[0], in1=tiles[1],
                                           op=ALU.add).then_inc(sum_step, 1)
                        return
                    for i in range(2):
                        pool.wait_ge(sum_step, 5 * g + 2 * p - 1 + i)
                        pool.tensor_tensor(out=psum_p[0:KP, :, :], in0=psum_p[0:KP, :, :], in1=tiles[i],
                                           op=ALU.add).then_inc(sum_step, 1)

                def add_bo():
                    for qt in range(QT):
                        pool.tensor_tensor(out=xb[0:QP, qt, :], in0=xb[0:QP, qt, :], in1=bo_s[0:QP, :],
                                           op=ALU.add).then_inc(bo_added, 1)

                for c in range(CC):
                    ctx_lo_part(0, c)
                pool.wait_ge(ctx_lo, CC)
                pool.memset(kst[ONES_ROW:P, :, :].bitcast(F32), 0.0).then_inc(cleared, 1)
                pool.wait_ge(cleared, 1)
                pool.memset(kst[ONES_ROW:ONES_ROW + 1, :, :].bitcast(F32), 1.0).then_inc(cleared, 1)
                pool.wait_ge(cleared, 2)

                def one(b, part, par):
                    for t in range(NG):
                        g = 4 * b + t
                        if has(part, t, "den"):
                            wait_full(pool, part, b, t, "den")
                        add_chunk(g, 0, (3 * t) % 2)
                        if t == 0 and part != "first":
                            pool.wait_ge(x_in, 16 * (2 * b + 1))
                            add_bo()
                        if t == 1 and part != "last":
                            ctx_lo_part(b + 1, 0)
                            ctx_lo_part(b + 1, 1)
                        add_chunk(g, 1, (3 * t + 1) % 2)
                        if t == 1 and part != "last":
                            ctx_lo_part(b + 1, 2)
                        add_chunk(g, 2, (3 * t + 2) % 2)

                batches(pool, one)
                pool.wait_ge(x_in, 16 * 2 * B)
                add_bo()

            @block.scalar
            def _(act):
                def w_split(dst, raw, scale, n):
                    act.wait_ge(w_in[n], 16)
                    act.activation(dst[:, :, :], raw.rearrange("p (c n) -> p c n", n=D), ACT.Copy,
                                   scale=scale).then_inc(w_hi, 1)

                def ctx_hi_part(b, c):
                    act.wait_ge(ctx_in[c], 16 * (b + 1))
                    act.activation(ctx_h[:, c, :], ctx_r[:, c % 2, :], ACT.Copy).then_inc(ctx_hi, 1)

                def xT_part(part, b, t, i):
                    bank = wait_full(act, part, b, t, f"xT{i}")
                    act.activation(xT_h[:, 2 * i:2 * i + 2, :],
                                   M[:, bank, 0:2 * NQ].rearrange("p (c n) -> p c n", c=2),
                                   ACT.Copy).then_inc(xT_hi, 1)

                def k_hi(part, b, t, kind, g, tg, i):
                    off, w = KHALF[i]
                    bank = wait_full(act, part, b, t, kind)
                    act.activation(kh_s[:, off:off + w], M[:, bank, 0:w], ACT.Identity,
                                   bias=bk_s[:, tg:tg + 1]).then_inc(kh_done, 1)

                def q_hi(part, b, t, kind, g, tg):
                    bank = wait_full(act, part, b, t, kind)
                    act.activation(qh_s[:, :], M[:, bank, 0:NQ], ACT.Identity,
                                   bias=bq_s[:, tg:tg + 1]).then_inc(qh_done, 1)

                def max_out(part, b, t):
                    bank, _ = misc(part, b, t, "mT")
                    wait_full(act, part, b, t, "mT")
                    act.activation(mneg[:, :], M[0:2 * GH, bank, 0:QP], ACT.Copy,
                                   scale=-1.0).then_inc(misc_free[bank], 1)

                def v_out(part, b, t, kind, kt, par):
                    bank = wait_full(act, part, b, t, kind)
                    act.activation(v01[0:KP, kt, :], M[0:KP, bank, 0:2 * P], ACT.Copy)
                    act.activation(v23[0:KP, par, kt, :], M[0:KP, bank, 2 * P:4 * P],
                                   ACT.Copy).then_inc(misc_free[bank], 1)

                w_split(wk_h, raw_k, 1.0, 0)
                ctx_hi_part(0, 0)
                ctx_hi_part(0, 1)
                w_split(wq_h, raw_q, SCALE, 1)
                w_split(wv_h, raw_v, 1.0, 2)
                act.wait_ge(ctx_lo, 1)
                ctx_hi_part(0, 2)
                xT_part("prologue", 0, 0, 0)
                xT_part("prologue", 0, 0, 1)
                w_split(wo_h, raw_o, 1.0, 3)
                act.wait_ge(consts, 3)
                for g in range(2):
                    if g:
                        act.wait_ge(kst_in, 48 * g)
                    k_hi("prologue", 0, 0, f"K0_{g}", g, g, 0)
                    k_hi("prologue", 0, 0, f"K1_{g}", g, g, 1)
                    if g:
                        act.wait_ge(qst_in, 48 * g)
                    q_hi("prologue", 0, 0, f"Q_{g}", g, g)
                act.wait_ge(w_lo, 4)
                for kt in range(KT):
                    if kt == KT - 1:
                        max_out("prologue", 0, 0)
                    v_out("prologue", 0, 0, f"V{kt}", kt, 0)

                def exps(g, t, part, p, j):
                    buf = (3 * t + p) % 2
                    n = 12 * g + 4 * p + j
                    if j == 0 and not (part == "first" and t == 0 and p < 2):
                        act.wait_ge(pv_done, 3 * g + p - 1)
                        act.wait_ge(sum_step, (5 * g - 2, 5 * g, 5 * g + 1)[p])
                    act.wait_ge(s_full, n + 1)
                    act.activation(pr[0:KP, buf, j, :, :],
                                   S[0:KP, (4 * p + j) % 3, 0:2 * NQ].rearrange("p (i n) -> p i n", i=2),
                                   ACT.Exp).then_inc(exp_done, 1)

                def o_copy(g):
                    act.wait_ge(pv_done, 3 * g + 3)
                    act.activation(o_s[:, :], O[:, 0:NQ], ACT.Copy).then_inc(ocopy_done, 1)

                def o_hi(g, t):
                    act.wait_ge(on_done, g + 1)
                    act.activation(oT_h[:, t, :], o_s[:, :], ACT.Identity, bias=bv_s[:, t:t + 1]).then_inc(oh_done, 1)

                def one(b, part, par):
                    for t in range(NG):
                        g = 4 * b + t
                        before = part != "first" or t > 0
                        project = has(part, t, "Q")
                        if before:
                            if part != "first" or t > 1:
                                act.wait_ge(ol_done, g - 1)
                            o_copy(g - 1)
                        if t == 2 and part != "last":
                            xT_part(part, b, t, 0)
                            xT_part(part, b, t, 1)
                        elif project:
                            act.wait_ge(qst_in, 48 * (g + 2))
                            q_hi(part, b, t, "Q", g + 2, (t + 2) % NG)
                        if project and t != 2:
                            act.wait_ge(kst_in, 48 * (g + 2))
                            k_hi(part, b, t, "K0", g + 2, (t + 2) % NG, 0)
                        exps(g, t, part, 0, 0)
                        exps(g, t, part, 0, 1)
                        if t == 2 and part != "last":
                            act.wait_ge(kst_in, 48 * (g + 2))
                            k_hi(part, b, t, "K0", g + 2, (t + 2) % NG, 0)
                            act.wait_ge(pv_done, 3 * g)
                            v_out(part, b, t, "V0", 0, 1 - par)
                        if t == 3 and part != "last":
                            v_out(part, b, t, "V3", 3, 1 - par)
                        exps(g, t, part, 0, 2)
                        exps(g, t, part, 0, 3)
                        if project and t == 2:
                            act.wait_ge(qst_in, 48 * (g + 2))
                            q_hi(part, b, t, "Q", g + 2, (t + 2) % NG)
                        if project:
                            k_hi(part, b, t, "K1", g + 2, (t + 2) % NG, 1)
                        exps(g, t, part, 1, 0)
                        if before:
                            if t == 1 and part != "first":
                                wait_full(act, part, b, 0, "O1")
                            o_hi(g - 1, (t - 1) % NG)
                        if t == 1 and part != "last":
                            wait_full(act, part, b, t, "K1")
                            ctx_hi_part(b + 1, 0)
                        exps(g, t, part, 1, 1)
                        if t == 1 and part != "last":
                            ctx_hi_part(b + 1, 1)
                        exps(g, t, part, 1, 2)
                        exps(g, t, part, 1, 3)
                        if t >= 2 and part != "last":
                            kt = 3 * (t - 2) + 1
                            v_out(part, b, t, f"V{kt}", kt, 1 - par)
                        exps(g, t, part, 2, 0)
                        exps(g, t, part, 2, 1)
                        exps(g, t, part, 2, 2)
                        exps(g, t, part, 2, 3)
                        if t == 1 and part != "last":
                            ctx_hi_part(b + 1, 2)
                        if t >= 2 and part != "last":
                            kt = 3 * (t - 2) + 2
                            v_out(part, b, t, f"V{kt}", kt, 1 - par)
                        if has(part, t, "mT"):
                            act.wait_ge(m_in, 16 * (g + 1))
                            max_out(part, b, t)

                batches(act, one)
                g = 4 * B - 1
                act.wait_ge(ol_done, g)
                o_copy(g)
                o_hi(g, NG - 1)

            @block.vector
            def _(dve):
                dve.memset(ones[:, :], 1.0).then_inc(consts, 1)
                dve.memset(qst[ONES_ROW:P, :, :].bitcast(F32), 0.0).then_inc(consts, 1)
                dve.wait_ge(c_in, 16 * 5)
                dve.tensor_scalar(bq_s[:, :], bq_s[:, :], SCALE, None, ALU.mult).then_inc(consts, 1)

                def w_rest(dst, hi, raw, scale, n):
                    dve.wait_ge(w_hi, n)
                    dve.scalar_tensor_tensor(out=dst[:, :, :], in0=raw.rearrange("p (c n) -> p c n", n=D),
                                             scalar=scale, in1=hi[:, :, :], op0=ALU.mult,
                                             op1=ALU.subtract).then_inc(w_lo, 1)

                def ln_stats(n):
                    for qt in range(QT):
                        dve.bn_stats(stats[0:QP, qt, :], xb[0:QP, qt, :]).then_inc(ln_stat, 1)
                    dve.wait_ge(ln_stat, QT * (n + 1))
                    dve.tensor_copy(settled[:, :], ones[:, 0:1])
                    for qt in range(QT):
                        dve.bn_aggr(mv[0:QP, qt, :], stats[0:QP, qt, :]).then_inc(ln_var, 1)

                def ln_rsqrt(n, first, last):
                    if first == 0:
                        dve.wait_ge(ln_var, QT * (n + 1))
                    rsqrt(dve, newton, RSQRT_STEPS * n, mv[0:QP, :, 1], EPS, ALU.add, ve[0:QP, :], rstd[0:QP, :],
                          rtmp[0:QP, :], first, last)

                def ln_apply(n):
                    for qt in range(QT):
                        dve.tensor_scalar(xb[0:QP, qt, :], xb[0:QP, qt, :], mv[0:QP, qt, 0:1],
                                          rstd[0:QP, qt:qt + 1], ALU.subtract, ALU.mult).then_inc(xn_done, 1)

                def xT_rest(part, b, t, i, n):
                    bank, _ = misc(part, b, t, f"xT{i}")
                    dve.wait_ge(xT_hi, n)
                    dve.tensor_tensor(out=xT_l[:, 2 * i:2 * i + 2, :],
                                      in0=M[:, bank, 0:2 * NQ].rearrange("p (c n) -> p c n", c=2),
                                      in1=xT_h[:, 2 * i:2 * i + 2, :],
                                      op=ALU.subtract).then_inc(misc_free[bank], 1)

                def k_lo(part, b, t, kind, g, tg, i):
                    off, w = KHALF[i]
                    bank, _ = misc(part, b, t, kind)
                    dve.wait_ge(kh_done, 2 * g + i + 1)
                    dve.scalar_tensor_tensor(out=kl_s[:, off:off + w], in0=M[:, bank, 0:w], scalar=bk_s[:, tg:tg + 1],
                                             in1=kh_s[:, off:off + w], op0=ALU.add,
                                             op1=ALU.subtract).then_inc(misc_free[bank], 1)

                def q_lo(part, b, t, kind, g, tg):
                    bank, _ = misc(part, b, t, kind)
                    dve.wait_ge(qh_done, g + 1)
                    dve.scalar_tensor_tensor(out=ql_s[:, :], in0=M[:, bank, 0:NQ], scalar=bq_s[:, tg:tg + 1],
                                             in1=qh_s[:, :], op0=ALU.add,
                                             op1=ALU.subtract).then_inc(misc_free[bank], 1)

                def maximum(g, u):
                    dve.wait_ge(x_full, 8 * g + u + 1)
                    dve.tensor_reduce(mx[0:QP, u:u + 1], X[0:QP, :, 0:HALF[0][1]], AX.XY,
                                      ALU.max).then_inc(max_done, 1)

                w_rest(wk_l, wk_h, raw_k, 1.0, 1)
                dve.wait_ge(x_in, 16)
                ln_stats(0)
                ln_rsqrt(0, 0, RSQRT_STEPS)
                ln_apply(0)
                w_rest(wq_l, wq_h, raw_q, SCALE, 2)
                xT_rest("prologue", 0, 0, 0, 1)
                xT_rest("prologue", 0, 0, 1, 2)
                w_rest(wv_l, wv_h, raw_v, 1.0, 3)
                w_rest(wo_l, wo_h, raw_o, 1.0, 4)
                for g in range(2):
                    if g:
                        dve.wait_ge(kst_in, 48 * g)
                    k_lo("prologue", 0, 0, f"K0_{g}", g, g, 0)
                    k_lo("prologue", 0, 0, f"K1_{g}", g, g, 1)
                    if g:
                        maximum(0, 0)
                        dve.wait_ge(qst_in, 48 * g)
                    q_lo("prologue", 0, 0, f"Q_{g}", g, g)
                for u in range(1, 2 * GH):
                    maximum(0, u)

                def normalise(part, b, t, g):
                    bank, count = misc(part, b, t, "den")
                    wait_full(dve, part, b, t, "den")
                    dve.reciprocal(rec[:, :], M[:, bank, 0:NQ]).then_inc(misc_free[bank], 1)
                    dve.wait_ge(misc_free[bank], count + 1)
                    dve.wait_ge(ocopy_done, g + 1)
                    dve.tensor_tensor(out=o_s[:, :], in0=o_s[:, :], in1=rec[:, :], op=ALU.mult).then_inc(on_done, 1)

                def o_lo(g, t):
                    dve.wait_ge(oh_done, g + 1)
                    dve.scalar_tensor_tensor(out=oT_l[:, t, :], in0=o_s[:, :], scalar=bv_s[:, t:t + 1],
                                             in1=oT_h[:, t, :], op0=ALU.add, op1=ALU.subtract).then_inc(ol_done, 1)

                def residual(part, b, t, qt, n):
                    bank = wait_full(dve, part, b, t, f"O{qt}")
                    dve.wait_ge(bo_added, QT * n + qt + 1)
                    dve.tensor_tensor(out=xb[0:QP, qt, :], in0=M[0:QP, bank, :], in1=xb[0:QP, qt, :],
                                      op=ALU.add).then_inc(misc_free[bank], 1)

                def one(b, part, par):
                    for t in range(NG):
                        g = 4 * b + t
                        before = part != "first" or t > 0
                        project = has(part, t, "Q")
                        ahead = has(part, t, "mT")
                        if ahead:
                            if t == 0 and part == "first":
                                wait_full(dve, "prologue", 0, 0, "mT")
                            elif t == 0:
                                wait_full(dve, "mid", b - 1, 3, "mT")
                            else:
                                wait_full(dve, part, b, t - 1, "mT")
                            maximum(g + 1, 0)
                        new = t == 2 and part != "last"
                        if new:
                            xT_rest(part, b, t, 0, 2 * (b + 1) + 1)
                        elif project:
                            dve.wait_ge(qst_in, 48 * (g + 2))
                            q_lo(part, b, t, "Q", g + 2, (t + 2) % NG)
                        if ahead:
                            maximum(g + 1, 1)
                        if new:
                            xT_rest(part, b, t, 1, 2 * (b + 1) + 2)
                        if project:
                            dve.wait_ge(kst_in, 48 * (g + 2))
                            k_lo(part, b, t, "K0", g + 2, (t + 2) % NG, 0)
                        if ahead:
                            maximum(g + 1, 2)
                        if before:
                            normalise(part, b, t, g - 1)
                        if ahead:
                            maximum(g + 1, 3)
                        if new:
                            dve.wait_ge(qst_in, 48 * (g + 2))
                            q_lo(part, b, t, "Q", g + 2, (t + 2) % NG)
                        if project:
                            k_lo(part, b, t, "K1", g + 2, (t + 2) % NG, 1)
                        ln = t == 1 and part != "last"
                        if ln:
                            dve.wait_ge(x_in, 16 * (2 * b + 2))
                            ln_stats(b + 1)
                        if ahead:
                            maximum(g + 1, 4)
                        if before:
                            o_lo(g - 1, (t - 1) % NG)
                        if ln:
                            ln_rsqrt(b + 1, 0, 4)
                        if ahead:
                            maximum(g + 1, 5)
                        if ln:
                            ln_rsqrt(b + 1, 4, 8)
                        if ahead:
                            maximum(g + 1, 6)
                        if ln:
                            ln_rsqrt(b + 1, 8, RSQRT_STEPS)
                            ln_apply(b + 1)
                        if t == 0 and part != "first":
                            residual(part, b, t, 0, b - 1)
                        if ahead:
                            maximum(g + 1, 7)
                        if t == 0 and part != "first":
                            residual(part, b, t, 1, b - 1)

                batches(dve, one)
                normalise("epilogue", 0, 0, 4 * B - 1)
                o_lo(4 * B - 1, NG - 1)
                for qt in range(QT):
                    residual("epilogue", 0, 0, qt, B - 1)

            @block.tensor
            def _(pe):
                def claim(part, b, t, kind):
                    bank, count = misc(part, b, t, kind)
                    if part != "prologue" or count > 0:
                        pe.wait_ge(misc_free[bank], count)
                    return bank, misc_full[bank]

                def transpose_x(part, b, t, i, n):
                    bank, full = claim(part, b, t, f"xT{i}")
                    pe.wait_ge(xn_done, QT * (n + 1))
                    for c in range(2):
                        for qt in range(QT):
                            o = c * NQ + qt * QP
                            last = pe.transpose(M[:, bank, o:o + QP], xb[0:QP, qt, P * (2 * i + c):P * (2 * i + c + 1)],
                                                id_s[0:QP, 0:QP])
                    last.then_inc(full, 1)

                def project_k(part, b, t, kind, tg, i):
                    off, w = KHALF[i]
                    bank, full = claim(part, b, t, kind)
                    cols = slice(P * tg, P * (tg + 1))
                    for c in range(CC):
                        last = split3(pe, M[:, bank, 0:w], (wk_h[:, c, cols], wk_l[:, c, cols]),
                                      (ctx_h[:, c, off:off + w], ctx_l[:, c, off:off + w]), c == 0, c == CC - 1)
                    last.then_inc(full, 1)

                def project_q(part, b, t, kind, tg):
                    bank, full = claim(part, b, t, kind)
                    cols = slice(P * tg, P * (tg + 1))
                    for c in range(DC):
                        last = split3(pe, M[:, bank, 0:NQ], (wq_h[:, c, cols], wq_l[:, c, cols]),
                                      (xT_h[:, c, :], xT_l[:, c, :]), c == 0, c == DC - 1)
                    last.then_inc(full, 1)

                def project_v(part, b, t, kind, kt):
                    bank, full = claim(part, b, t, kind)
                    keys = slice(KP * kt, KP * (kt + 1))
                    for c in range(CC):
                        last = split3(pe, M[0:KP, bank, :], (ctx_h[:, c, keys], ctx_l[:, c, keys]),
                                      (wv_h[:, c, :], wv_l[:, c, :]), c == 0, c == CC - 1)
                    last.then_inc(full, 1)

                def score_for_max(g, tg, u, first=False):
                    h, qt = GH * tg + u // QT, u % QT
                    if u == 0:
                        pe.wait_ge(kst_in, 48 * (g + 1))
                        pe.wait_ge(qst_in, 48 * (g + 1))
                    if not (first and u == 0):
                        pe.wait_ge(max_done, 8 * g + u)
                    for i, (off, w) in enumerate(HALF):
                        last = pe.matmul(X[0:QP, i, 0:w], qst[0:ONES_ROW, h, QP * qt:QP * (qt + 1)],
                                         kst[0:ONES_ROW, h, off:off + w], start=True, stop=True)
                    last.then_inc(x_full, 1)

                def transpose_max(part, b, t, g):
                    bank, full = claim(part, b, t, "mT")
                    pe.wait_ge(max_done, 8 * (g + 1))
                    pe.transpose(M[0:2 * GH, bank, 0:QP], mx[0:QP, :], id_s[0:QP, 0:QP]).then_inc(full, 1)

                pe.wait_ge(c_in, 16 * 5)
                transpose_x("prologue", 0, 0, 0, 0)
                transpose_x("prologue", 0, 0, 1, 0)
                pe.wait_ge(ctx_lo, CC)
                pe.wait_ge(w_lo, 1)
                for g in range(2):
                    project_k("prologue", 0, 0, f"K0_{g}", g, 0)
                    project_k("prologue", 0, 0, f"K1_{g}", g, 1)
                    if g == 0:
                        pe.wait_ge(w_lo, 2)
                    else:
                        score_for_max(0, 0, 0, True)
                    project_q("prologue", 0, 0, f"Q_{g}", g)
                pe.wait_ge(w_lo, 3)
                for u in range(1, 2 * GH):
                    score_for_max(0, 0, u, True)
                    if u < KT:
                        project_v("prologue", 0, 0, f"V{u - 1}", u - 1)
                transpose_max("prologue", 0, 0, 0)
                project_v("prologue", 0, 0, f"V{KT - 1}", KT - 1)
                pe.wait_ge(w_lo, 4)
                wait_freed(pe, "prologue", 0, 0, "mT", "V5")
                pe.wait_ge(consts, 3)
                pe.wait_ge(cleared, 2)

                def score(g, t, part, p, j):
                    n = 12 * g + 4 * p + j
                    if not (part == "first" and t == 0 and 4 * p + j < 3):
                        pe.wait_ge(exp_done, n - 2)
                    for i in range(2):
                        o = KP * (2 * p + i)
                        last = pe.matmul(S[0:KP, (4 * p + j) % 3, NQ * i:NQ * (i + 1)],
                                         kst[:, GH * t + j, o:o + KP], qst[:, GH * t + j, :], start=True, stop=True)
                    last.then_inc(s_full, 1)

                def values(g, t, par, p):
                    pe.wait_ge(exp_done, 12 * g + 4 * p + 4)
                    v = v_of(t, par)
                    for i in range(2):
                        for j in range(GH):
                            last = pe.matmul(O[HD * j:HD * (j + 1), 0:NQ], v[0:KP, 2 * p + i, HD * j:HD * (j + 1)],
                                             pr[0:KP, (3 * t + p) % 2, j, i, :], start=(p == 0 and i == 0),
                                             stop=(p == 2 and i == 1))
                    last.then_inc(pv_done, 1)

                def denominators(part, b, t, g):
                    bank, full = claim(part, b, t, "den")
                    pe.wait_ge(sum_step, 5 * (g + 1))
                    for j in range(GH):
                        last = pe.matmul(M[HD * j:HD * (j + 1), bank, 0:NQ], ones[0:KP, :], psum_p[0:KP, j, :],
                                         start=True, stop=True)
                    last.then_inc(full, 1)

                def project_o(part, b, t, qt, n):
                    bank, full = claim(part, b, t, f"O{qt}")
                    pe.wait_ge(ol_done, NG * n)
                    rows = slice(QP * qt, QP * (qt + 1))
                    for c in range(NG):
                        last = split3(pe, M[0:QP, bank, :], (oT_h[:, c, rows], oT_l[:, c, rows]),
                                      (wo_h[:, c, :], wo_l[:, c, :]), c == 0, c == NG - 1)
                    last.then_inc(full, 1)

                def one(b, part, par):
                    for t in range(NG):
                        g = 4 * b + t
                        before = part != "first" or t > 0
                        project = has(part, t, "Q")
                        ahead = has(part, t, "mT")
                        tn = (t + 1) % NG

                        def for_max(u):
                            if ahead:
                                score_for_max(g + 1, tn, u)

                        for_max(0)
                        if before:
                            values(g - 1, (t - 1) % NG, par if t else 1 - par, 2)
                        new = t == 2 and part != "last"
                        if new:
                            transpose_x(part, b, t, 0, b + 1)
                            transpose_x(part, b, t, 1, b + 1)
                        elif project:
                            project_q(part, b, t, "Q", (t + 2) % NG)
                        for_max(1)
                        if project and not new:
                            project_k(part, b, t, "K0", (t + 2) % NG, 0)
                        pe.wait_ge(m_in, 16 * (g + 1))
                        score(g, t, part, 0, 0)
                        score(g, t, part, 0, 1)
                        if new:
                            pe.wait_ge(ctx_lo, CC * (b + 2))
                            project_k(part, b, t, "K0", (t + 2) % NG, 0)
                        for_max(2)
                        if t == 2 and part != "last":
                            project_v(part, b, t, "V0", 0)
                        if t == 3 and part != "last":
                            project_v(part, b, t, "V3", 3)
                        score(g, t, part, 0, 2)
                        if before:
                            denominators(part, b, t, g - 1)
                        for_max(3)
                        score(g, t, part, 0, 3)
                        if new:
                            project_q(part, b, t, "Q", (t + 2) % NG)
                        if project:
                            project_k(part, b, t, "K1", (t + 2) % NG, 1)
                        score(g, t, part, 1, 0)
                        for_max(4)
                        if before:
                            pe.wait_ge(ocopy_done, g)
                        if t == 0 and part != "first":
                            wait_freed(pe, "mid", b - 1, 3, "V4", "V5")
                        values(g, t, par, 0)
                        score(g, t, part, 1, 1)
                        for_max(5)
                        score(g, t, part, 1, 2)
                        score(g, t, part, 1, 3)
                        if t == 0 and part != "first":
                            project_o(part, b, t, 0, b)
                        if t >= 2 and part != "last":
                            kt = 3 * (t - 2) + 1
                            project_v(part, b, t, f"V{kt}", kt)
                        for_max(6)
                        score(g, t, part, 2, 0)
                        values(g, t, par, 1)
                        score(g, t, part, 2, 1)
                        for_max(7)
                        score(g, t, part, 2, 2)
                        score(g, t, part, 2, 3)
                        if t == 0 and part != "first":
                            project_o(part, b, t, 1, b)
                        if t >= 2 and part != "last":
                            kt = 3 * (t - 2) + 2
                            project_v(part, b, t, f"V{kt}", kt)
                        if ahead:
                            transpose_max(part, b, t, g + 1)

                batches(pe, one)
                values(4 * B - 1, NG - 1, 1, 2)
                denominators("epilogue", 0, 0, 4 * B - 1)
                for qt in range(QT):
                    project_o("epilogue", 0, 0, qt, B)


E, DE = 8, 256
NE = D // P
TB = 512
NB = B * NQ // TB
FT = E * DE // P
NORM_EPS2 = 1e-24
PREP_UNITS = 6
LOGITS, GATES = 4, 5
PREP_DELAY = 2
ROUTE_STEPS, ROUTE_EX = 13, 8


def expert_phase(nc, x1, w1, b1, w2, b2, centroids, w_route, ident, gates_dram, out):
    with ExitStack() as es:
        def sb(name, shape, dt=F32):
            return es.enter_context(nc.sbuf_tensor(name, shape, dt))

        def sem(name):
            return es.enter_context(nc.semaphore(name))

        w1_h, w1_l = sb("w1_h", [P, E, DC, DE], F32R), sb("w1_l", [P, E, DC, DE], F32R)
        w2_h, w2_l = sb("w2_h", [P, E, 2, D], F32R), sb("w2_l", [P, E, 2, D], F32R)
        b1_s, b2_s = sb("b1_s", [P, FT]), sb("b2_s", [E, D])
        id_s = sb("id2_s", [P, P])
        css, cve, cinv, ctmp = sb("css", [E, 1]), sb("cve", [E, 1]), sb("cinv", [E, 1]), sb("ctmp", [E, 1])
        rw = sb("rw", [P, DC, 4 * E], F32R)
        xt = sb("xt", [P, NE, TB])
        res = sb("res", [P, NE, TB])
        xT_h, xT_l = sb("bxT_h", [P, 2, DC, TB], F32R), sb("bxT_l", [P, 2, DC, TB], F32R)
        gate_b = sb("gate_b", [P, 4, TB])
        hid = sb("hid", [P, 2, TB])
        hid_h, hid_l = sb("hid_h", [P, 2, TB], F32R), sb("hid_l", [P, 2, TB], F32R)
        squares = sb("squares", [P, TB])
        stats, mv, rstd = sb("bstats", [P, NE, 6]), sb("bmv", [P, NE, 2]), sb("brstd", [P, NE])
        ve, rtmp, settled = sb("bve", [P, NE]), sb("brtmp", [P, NE]), sb("bsettled", [P, 1])
        ss, rinv = sb("ss", [P, NE]), sb("rinv", [P, NE])
        lg_lo, lg = sb("lg_lo", [P, NE, 2 * E]), sb("lg", [P, NE, 2 * E])
        logit, top8 = sb("logit", [P, NE, E]), sb("top8", [P, NE, 8])
        mask, ex, gsum, gates = sb("mask", [P, NE, E]), sb("ex", [P, NE, E]), sb("gsum", [P, NE]), sb("gates", [P, NE, E])
        gT = sb("gT", [E, TB])
        cent, wr = gate_b[0:E, 0, :], gate_b[0:E, 1, :]

        Y = es.enter_context(nc.psum_tensor("Y", [P, NE, 512], F32))
        HP = es.enter_context(nc.psum_tensor("HP", [P, 2, 512], F32))
        M = es.enter_context(nc.psum_tensor("PREP", [P, 2, 512], F32))

        c_in = sem("c_in")
        w_in = [sem("ew_in0"), sem("ew_in1")]
        w_hi, w_lo = sem("ew_hi"), sem("ew_lo")
        cent_ss, cent_step = sem("cent_ss"), sem("cent_step")
        rw_hi = sem("rw_hi")
        x_in, r_in = sem("ex_in"), sem("r_in")
        out_done = sem("out_done")
        ln_stat, ln_var, newton = sem("eln_stat"), sem("eln_var"), sem("enewton")
        xn_done = sem("exn_done")
        ss_done = sem("ss_done")
        prep_full = [sem("prep_full0"), sem("prep_full1")]
        prep_free = [sem("prep_free0"), sem("prep_free1")]
        xT_hi = sem("exT_hi")
        route, ex_done = sem("route"), sem("ex_done")
        gT_out = sem("gT_out")
        gate_in = [sem(f"gate_in{i}") for i in range(4)]
        h_full, gelu_done, gated = sem("h_full"), sem("gelu_done"), sem("gated")
        hh_done, hl_done = sem("hh_done"), sem("hl_done")
        y_done, y_read = sem("y_done"), sem("y_read")

        x1v = x1.rearrange("(k m p) d -> k p m d", m=NE, p=P)
        outv = out.rearrange("(k m p) d -> k p m d", m=NE, p=P)
        res_flat = res[:].rearrange("p m n -> p (m n)")
        pieces = []
        for e in range(E):
            for i, (w, hi, lo, n) in enumerate(((w1, w1_h, w1_l, DE), (w2, w2_h, w2_l, D))):
                slot = res_flat[:, 2 * D * i:2 * D * (i + 1)].rearrange("p (c n) -> p c n", n=n)
                pieces.append((w[e].rearrange("(c p) n -> p c n", p=P), hi[:, e], lo[:, e], slot))

        def prep(k, u):
            return u % 2, 1 + (PREP_UNITS // 2) * k + u // 2

        def prep_filled(eng, k, u):
            bank, count = prep(k, u)
            eng.wait_ge(prep_full[bank], count + 1)
            return bank

        def prep_freed(eng, k, u):
            bank, count = prep(k, u)
            eng.wait_ge(prep_free[bank], count + 1)

        def blocks(eng, one):
            one(0, 0, "first")
            with eng.Fori(0, (NB - 3) // 2) as pair:
                one(pair * 2 + 1, 1, "mid")
                one(pair * 2 + 2, 0, "mid")
            one(NB - 2, 1, "mid")
            one(NB - 1, 0, "last")

        with nc.Block() as block:

            @block.sync
            def _(sp):
                def load_w(n):
                    src, _, _, slot = pieces[n]
                    sp.dma_start(slot, src).then_inc(w_in[n % 2], 16)

                def load_gates(k, e):
                    sp.dma_start(gate_b[:, e % 4, :], gates_dram[k, e].partition_broadcast(P)).then_inc(gate_in[e % 4], 16)

                sp.dma_start(xt[:, :, :], x1v[0]).then_inc(x_in, 16)
                for dst, src in ((cent, centroids), (wr, w_route), (id_s[:, :], ident), (b1_s[:, :], b1), (b2_s[:, :], b2)):
                    sp.dma_start(dst, src).then_inc(c_in, 16)
                load_w(0)
                load_w(1)
                for n in range(2, 6):
                    sp.wait_ge(w_hi, n - 1)
                    sp.wait_ge(w_lo, n - 1)
                    load_w(n)
                prep_freed(sp, 0, GATES)
                sp.dma_start(gates_dram[0], gT[:, :]).then_inc(gT_out, 16)
                sp.wait_ge(gT_out, 16)
                for e in range(4):
                    load_gates(0, e)

                def one(k, par, part):
                    if part == "first":
                        prep_filled(sp, k, DC - 1)
                        sp.wait_ge(ss_done, NE * (k + 1))
                        sp.dma_start(xt[:, :, :], x1v[k + 1]).then_inc(x_in, 16)
                        for n in range(6, len(pieces)):
                            sp.wait_ge(w_hi, n - 1)
                            sp.wait_ge(w_lo, n - 1)
                            load_w(n)
                            if n % 2 and n // 2 + 1 < E:
                                e = n // 2 + 1
                                sp.wait_ge(gated, 2 * (e - 3))
                                load_gates(k, e)
                        sp.wait_ge(w_hi, len(pieces))
                        sp.wait_ge(w_lo, len(pieces))
                        sp.dma_start(res[:, :, :], x1v[0]).then_inc(r_in, 16)
                    else:
                        if part == "mid":
                            bank, count = prep(k, DC - 1)
                            wait_all(sp, (prep_full[bank], count + 1), (ss_done, NE * (k + 1)))
                            sp.dma_start(xt[:, :, :], x1v[k + 1]).then_inc(x_in, 16)
                        sp.wait_ge(out_done, 16 * k)
                        sp.dma_start(res[:, :, :], x1v[k]).then_inc(r_in, 16)
                        for e in range(4, E):
                            sp.wait_ge(gated, FT * k + 2 * (e - 3))
                            load_gates(k, e)
                    if part != "last":
                        prep_freed(sp, k + 1, GATES)
                        sp.dma_start(gates_dram[k + 1], gT[:, :]).then_inc(gT_out, 16)
                        for e in range(4):
                            wait_all(sp, *([(gT_out, 16 * (k + 2))] if e == 0 else []), (gated, FT * k + 2 * (e + 5)))
                            load_gates(k + 1, e)
                    sp.wait_ge(y_read, NE * (k + 1))
                    sp.dma_start(outv[k], res[:, :, :]).then_inc(out_done, 16)

                blocks(sp, one)
                sp.wait_ge(out_done, 16 * NB)

            @block.scalar
            def _(act):
                def w_part(n):
                    _, hi, _, slot = pieces[n]
                    act.wait_ge(w_in[n % 2], 16 * (n // 2 + 1))
                    act.activation(hi, slot, ACT.Copy).then_inc(w_hi, 1)

                def square(k, m, first=False):
                    act.wait_ge(xn_done, NE * k + m + 1)
                    if first:
                        act.wait_ge(cent_ss, 1)
                    else:
                        act.wait_ge(ss_done, NE * k + m)
                    act.activation(squares[:, :], xt[:, m, :], ACT.Square,
                                   accum_out=ss[:, m:m + 1]).then_inc(ss_done, 1)

                def xT_part(k, par, u):
                    bank = prep_filled(act, k, u)
                    act.activation(xT_h[:, par, u, :], M[:, bank, :], ACT.Copy).then_inc(xT_hi, 1)

                def exps(k):
                    act.wait_ge(route, ROUTE_STEPS * k + ROUTE_EX)
                    act.activation(ex[:, :, :], ex[:, :, :], ACT.Exp).then_inc(ex_done, 1)

                def gT_part(k):
                    bank = prep_filled(act, k, GATES)
                    act.activation(gT[:, :], M[0:E, bank, :], ACT.Copy).then_inc(prep_free[bank], 1)

                act.wait_ge(c_in, 16 * 5)
                act.activation(squares[0:E, :], cent, ACT.Square, accum_out=css[:, :]).then_inc(cent_ss, 1)
                w_part(0)
                w_part(1)
                for i in range(2):
                    act.wait_ge(prep_full[i], 1)
                    act.activation(rw[:, :, E * i:E * (i + 1)],
                                   M[:, i, 0:DC * E].rearrange("p (c e) -> p c e", e=E), ACT.Copy).then_inc(rw_hi, 1)
                for u in range(DC):
                    xT_part(0, 0, u)
                for m in range(NE):
                    square(0, m, m == 0)
                w_part(2)
                w_part(3)
                exps(0)
                gT_part(0)

                def gelu(k, f):
                    act.wait_ge(h_full, FT * k + f + 1)
                    act.activation(hid[:, f % 2, :], HP[:, f % 2, :], ACT.Gelu,
                                   bias=b1_s[:, f:f + 1]).then_inc(gelu_done, 1)

                def hid_hi(k, f):
                    act.wait_ge(gated, FT * k + f + 1)
                    act.activation(hid_h[:, f % 2, :], hid[:, f % 2, :], ACT.Copy).then_inc(hh_done, 1)

                def one(k, par, part):
                    ahead = part != "last"
                    for f in range(FT):
                        step = f - PREP_DELAY
                        n = FT * k + f
                        if part != "first" or f >= 2:
                            act.wait_ge(hl_done, n - 1)
                        gelu(k, f)
                        if f:
                            if part != "first" or f >= 3:
                                act.wait_ge(y_done, n - 2)
                            hid_hi(k, f - 1)
                        if part == "first" and f % 2 == 0 and f // 2 + 2 < E:
                            w_part(f + 4)
                            w_part(f + 5)
                        if ahead and step == 1:
                            for m in range(NE):
                                square(k + 1, m)
                        if ahead and step in (2, 3):
                            xT_part(k + 1, 1 - par, 2 * step - 4)
                            xT_part(k + 1, 1 - par, 2 * step - 3)
                        if ahead and step == 8:
                            exps(k + 1)
                        if ahead and step == 11:
                            act.wait_ge(gT_out, 16 * (k + 1))
                            gT_part(k + 1)
                    act.wait_ge(y_done, FT * k + FT - 2)
                    hid_hi(k, FT - 1)

                blocks(act, one)

            @block.vector
            def _(dve):
                def w_rest(n):
                    _, hi, lo, slot = pieces[n]
                    dve.wait_ge(w_hi, n + 1)
                    dve.tensor_tensor(out=lo, in0=slot, in1=hi, op=ALU.subtract).then_inc(w_lo, 1)

                def ln_stats(k):
                    dve.wait_ge(x_in, 16 * (k + 1))
                    for m in range(NE):
                        dve.bn_stats(stats[:, m, :], xt[:, m, :]).then_inc(ln_stat, 1)
                    dve.wait_ge(ln_stat, NE * (k + 1))
                    dve.tensor_copy(settled[:, :], id_s[:, 0:1])
                    for m in range(NE):
                        dve.bn_aggr(mv[:, m, :], stats[:, m, :]).then_inc(ln_var, 1)

                def ln_apply(k):
                    dve.wait_ge(ln_var, NE * (k + 1))
                    rsqrt(dve, newton, RSQRT_STEPS * (2 * k + 1), mv[:, :, 1], EPS, ALU.add,
                          ve[:, :], rstd[:, :], rtmp[:, :])
                    for m in range(NE):
                        dve.tensor_scalar(xt[:, m, :], xt[:, m, :], mv[:, m, 0:1], rstd[:, m:m + 1],
                                          ALU.subtract, ALU.mult).then_inc(xn_done, 1)

                def xT_rest(k, par, u):
                    bank, _ = prep(k, u)
                    dve.wait_ge(xT_hi, DC * k + u + 1)
                    dve.tensor_tensor(out=xT_l[:, par, u, :], in0=M[:, bank, :], in1=xT_h[:, par, u, :],
                                      op=ALU.subtract).then_inc(prep_free[bank], 1)

                def each(ap):
                    return ap.broadcast_to([P, NE, E])

                def route_before(k):
                    done = ROUTE_STEPS * k
                    dve.wait_ge(ss_done, NE * (k + 1))
                    rsqrt(dve, newton, RSQRT_STEPS * (2 * k + 2), ss[:, :], NORM_EPS2, ALU.max,
                          ve[:, :], rinv[:, :], rtmp[:, :])
                    bank = prep_filled(dve, k, LOGITS)
                    _, count = prep(k, LOGITS)
                    L = M[:, bank, 0:NE * 4 * E].rearrange("p (m e) -> p m e", m=NE)
                    dve.tensor_copy(lg_lo[:, :, :], L[:, :, 2 * E:4 * E]).then_inc(route, 1)
                    dve.wait_ge(route, done + 1)
                    dve.tensor_tensor(out=lg[:, :, :], in0=L[:, :, 0:2 * E], in1=lg_lo[:, :, :],
                                      op=ALU.add).then_inc(prep_free[bank], 1)
                    dve.wait_ge(prep_free[bank], count + 1)
                    dve.tensor_tensor(out=logit[:, :, :], in0=lg[:, :, E:2 * E], in1=each(rinv[:, :].unsqueeze(2)),
                                      op=ALU.mult).then_inc(route, 1)
                    dve.wait_ge(route, done + 2)
                    dve.tensor_tensor(out=logit[:, :, :], in0=logit[:, :, :], in1=lg[:, :, 0:E],
                                      op=ALU.add).then_inc(route, 1)
                    dve.wait_ge(route, done + 3)
                    dve.tensor_copy(settled[:, :], id_s[:, 0:1])
                    for m in range(NE):
                        dve.max(top8[:, m, :], logit[:, m, :]).then_inc(route, 1)
                    dve.wait_ge(route, done + 7)
                    dve.tensor_tensor(out=ex[:, :, :], in0=logit[:, :, :], in1=each(top8[:, :, 0:1]),
                                      op=ALU.subtract).then_inc(route, 1)
                    dve.tensor_tensor(out=mask[:, :, :], in0=logit[:, :, :], in1=each(top8[:, :, 1:2]),
                                      op=ALU.is_ge).then_inc(route, 1)

                def route_after(k):
                    done = ROUTE_STEPS * k + 9
                    dve.wait_ge(ex_done, k + 1)
                    dve.wait_ge(route, done)
                    dve.tensor_tensor(out=ex[:, :, :], in0=ex[:, :, :], in1=mask[:, :, :], op=ALU.mult).then_inc(route, 1)
                    dve.wait_ge(route, done + 1)
                    dve.tensor_reduce(gsum[:, :], ex[:, :, :], AX.X, ALU.add).then_inc(route, 1)
                    dve.wait_ge(route, done + 2)
                    dve.reciprocal(gsum[:, :], gsum[:, :]).then_inc(route, 1)
                    dve.wait_ge(route, done + 3)
                    dve.tensor_tensor(out=gates[:, :, :], in0=ex[:, :, :], in1=each(gsum[:, :].unsqueeze(2)),
                                      op=ALU.mult).then_inc(route, 1)

                dve.wait_ge(cent_ss, 1)
                rsqrt(dve, newton, 0, css[:, :], NORM_EPS2, ALU.max, cve[:, :], cinv[:, :], ctmp[:, :])
                dve.tensor_scalar(cent, cent, cinv[:, 0:1], None, ALU.mult).then_inc(cent_step, 1)
                ln_stats(0)
                ln_apply(0)
                for i in range(2):
                    dve.wait_ge(rw_hi, i + 1)
                    dve.tensor_tensor(out=rw[:, :, E * (2 + i):E * (3 + i)],
                                      in0=M[:, i, 0:DC * E].rearrange("p (c e) -> p c e", e=E),
                                      in1=rw[:, :, E * i:E * (i + 1)], op=ALU.subtract).then_inc(prep_free[i], 1)
                w_rest(0)
                for u in range(DC):
                    xT_rest(0, 0, u)
                w_rest(1)
                w_rest(2)
                w_rest(3)
                route_before(0)
                route_after(0)

                def gate(k, f):
                    e = f // 2
                    dve.wait_ge(gelu_done, FT * k + f + 1)
                    if f % 2 == 0:
                        dve.wait_ge(gate_in[e % 4], 16 * (2 * k + e // 4 + 1))
                    dve.tensor_tensor(out=hid[:, f % 2, :], in0=hid[:, f % 2, :], in1=gate_b[:, e % 4, :],
                                      op=ALU.mult).then_inc(gated, 1)

                def hid_lo(k, f):
                    dve.wait_ge(hh_done, FT * k + f + 1)
                    dve.tensor_tensor(out=hid_l[:, f % 2, :], in0=hid[:, f % 2, :], in1=hid_h[:, f % 2, :],
                                      op=ALU.subtract).then_inc(hl_done, 1)

                def one(k, par, part):
                    ahead = part != "last"
                    for f in range(FT):
                        step = f - PREP_DELAY
                        gate(k, f)
                        if f:
                            hid_lo(k, f - 1)
                        if part == "first" and f % 2 == 0 and f // 2 + 2 < E:
                            w_rest(f + 4)
                            w_rest(f + 5)
                        if ahead and step == 0:
                            ln_stats(k + 1)
                        if ahead and step == 1:
                            ln_apply(k + 1)
                        if ahead and step in (3, 4):
                            xT_rest(k + 1, 1 - par, 2 * step - 6)
                            xT_rest(k + 1, 1 - par, 2 * step - 5)
                        if ahead and step == 7:
                            route_before(k + 1)
                        if ahead and step == 9:
                            route_after(k + 1)
                    hid_lo(k, FT - 1)
                    dve.wait_ge(y_done, FT * (k + 1))
                    dve.wait_ge(r_in, 16 * (k + 1))
                    for m in range(NE):
                        dve.tensor_tensor(out=res[:, m, :], in0=Y[:, m, :], in1=res[:, m, :],
                                          op=ALU.add).then_inc(y_read, 1)

                blocks(dve, one)

            @block.tensor
            def _(pe):
                def transpose_x(k, u):
                    bank, count = prep(k, u)
                    pe.wait_ge(prep_free[bank], count)
                    pe.wait_ge(xn_done, NE * (k + 1))
                    for m in range(NE):
                        last = pe.transpose(M[:, bank, P * m:P * (m + 1)], xt[:, m, P * u:P * (u + 1)], id_s[:, :])
                    last.then_inc(prep_full[bank], 1)

                def logits(k, par):
                    bank, count = prep(k, LOGITS)
                    pe.wait_ge(prep_free[bank], count)
                    prep_freed(pe, k, DC - 1)
                    for m in range(NE):
                        tokens = slice(P * m, P * (m + 1))
                        o = 4 * E * m
                        for c in range(DC):
                            pe.matmul(M[:, bank, o:o + 4 * E], xT_h[:, par, c, tokens], rw[:, c, :],
                                      start=c == 0, stop=False)
                            last = pe.matmul(M[:, bank, o:o + 2 * E], xT_l[:, par, c, tokens], rw[:, c, 0:2 * E],
                                             start=False, stop=c == DC - 1)
                    last.then_inc(prep_full[bank], 1)

                def transpose_gates(k):
                    bank, count = prep(k, GATES)
                    pe.wait_ge(prep_free[bank], count)
                    pe.wait_ge(route, ROUTE_STEPS * (k + 1))
                    for m in range(NE):
                        last = pe.transpose(M[0:E, bank, P * m:P * (m + 1)], gates[:, m, :], id_s[:, :])
                    last.then_inc(prep_full[bank], 1)

                pe.wait_ge(c_in, 16 * 5)
                for i, src in enumerate((wr, cent)):
                    if i:
                        pe.wait_ge(cent_step, 1)
                    for c in range(DC):
                        last = pe.transpose(M[:, i, E * c:E * (c + 1)], src[:, P * c:P * (c + 1)], id_s[0:E, 0:E])
                    last.then_inc(prep_full[i], 1)

                def up(k, par, f, part):
                    n, e, cols = FT * k + f, f // 2, slice(P * (f % 2), P * (f % 2 + 1))
                    if part != "first" or f >= 2:
                        pe.wait_ge(gelu_done, n - 1)
                    if part == "first" and f % 2 == 0:
                        pe.wait_ge(w_lo, f + 1)
                    for c in range(DC):
                        out_ap = HP[:, f % 2, :]
                        pe.matmul(out_ap, w1_h[:, e, c, cols], xT_h[:, par, c, :], start=c == 0, stop=False)
                        pe.matmul(out_ap, w1_h[:, e, c, cols], xT_l[:, par, c, :], start=False, stop=False)
                        last = pe.matmul(out_ap, w1_l[:, e, c, cols], xT_h[:, par, c, :], start=False, stop=c == DC - 1)
                    last.then_inc(h_full, 1)

                def down(k, f, part):
                    e, j = f // 2, f % 2
                    if f == 0:
                        prep_freed(pe, k, GATES)
                        for m in range(NE):
                            if part != "first":
                                pe.wait_ge(y_read, NE * (k - 1) + m + 1)
                            pe.matmul(Y[:, m, :], gT[:, P * m:P * (m + 1)], b2_s[:, :], start=True, stop=False)
                    if part == "first" and f % 2 == 0:
                        pe.wait_ge(w_lo, f + 2)
                    pe.wait_ge(hl_done, FT * k + f + 1)
                    for m in range(NE):
                        tokens = slice(P * m, P * (m + 1))
                        pe.matmul(Y[:, m, :], hid_h[:, f % 2, tokens], w2_h[:, e, j, :], start=False, stop=False)
                        pe.matmul(Y[:, m, :], hid_h[:, f % 2, tokens], w2_l[:, e, j, :], start=False, stop=False)
                        last = pe.matmul(Y[:, m, :], hid_l[:, f % 2, tokens], w2_h[:, e, j, :], start=False,
                                         stop=f == FT - 1)
                    last.then_inc(y_done, 1)

                for u in range(DC):
                    transpose_x(0, u)
                logits(0, 0)
                up(0, 0, 0, "first")
                transpose_gates(0)

                def one(k, par, part):
                    ahead = part != "last"
                    for f in range(FT):
                        step = f - PREP_DELAY
                        if f:
                            up(k, par, f, part)
                        if f > 1:
                            down(k, f - 2, part)
                        if ahead and step in (2, 3):
                            transpose_x(k + 1, 2 * step - 4)
                            transpose_x(k + 1, 2 * step - 3)
                        if ahead and step == 6:
                            logits(k + 1, 1 - par)
                        if ahead and step == 10:
                            transpose_gates(k + 1)
                    down(k, FT - 2, part)
                    if ahead:
                        up(k + 1, 1 - par, 0, "mid")
                    down(k, FT - 1, part)

                blocks(pe, one)


def kernel(**inputs):
    import concourse.bacc as _bacc
    import numpy as np
    from concourse import mybir as _mybir
    from concourse.bass_utils import run_bass_kernel_spmd as _run

    order = np.arange(D).reshape(NG, GH, HD).transpose(0, 2, 1).reshape(-1)
    put = {
        "x": inputs["x"].reshape(B * NQ, D),
        "ctxT": inputs["ctx_768"].transpose(0, 2, 1),
        "wqT": inputs["L0_xattn_Wq"].T[:, order],
        "bq": inputs["L0_xattn_bq"][order].reshape(NG, P).T,
        "wkT": inputs["L0_xattn_Wk"].T[:, order],
        "bk": inputs["L0_xattn_bk"][order].reshape(NG, P).T,
        "wvT": inputs["L0_xattn_Wv"].T,
        "bv": inputs["L0_xattn_bv"].reshape(NG, P).T,
        "woT": inputs["L0_xattn_Wo"].T,
        "bo": inputs["L0_xattn_bo"],
        "ident": np.eye(P, dtype=np.float32),
        "w1": inputs["L0_ffn_w1"],
        "b1": inputs["L0_ffn_b1"].reshape(FT, P).T,
        "w2": inputs["L0_ffn_w2"],
        "b2": inputs["L0_ffn_b2"],
        "centroids": inputs["L0_ffn_centroids"],
        "w_route": inputs["L0_ffn_w_route"],
    }
    put = {name: np.ascontiguousarray(a) for name, a in put.items()}
    nc = _bacc.Bacc("TRN2", target_bir_lowering=False, num_devices=1)
    ap = {name: nc.dram_tensor(name, a.shape, _mybir.dt.from_np(a.dtype), kind="ExternalInput").ap()
          for name, a in put.items()}
    out = nc.dram_tensor("out", (B * NQ, D), F32, kind="ExternalOutput").ap()
    x1 = nc.dram_tensor("x1", (B * NQ, D), F32, kind="Internal").ap()
    gates = nc.dram_tensor("gates_dram", (NB, E, TB), F32, kind="Internal").ap()
    attention_phase(nc, *(ap[n] for n in ("x", "ctxT", "wqT", "bq", "wkT", "bk", "wvT", "bv", "woT", "bo", "ident")), x1)
    expert_phase(nc, x1, *(ap[n] for n in ("w1", "b1", "w2", "b2", "centroids", "w_route", "ident")), gates, out)
    got = _run(nc, [put], core_ids=[0]).results[0]["out"]
    return got.reshape(B, NQ, D)
```
